# Optimizing a Trainium2 kernel written in Bass

```python
import numpy as np
import jax
import jax.numpy as jnp

def _softmax(x, axis=-1):
    return jax.nn.softmax(x, axis=axis)

def _gelu(x):
    return jax.nn.gelu(x, approximate=True)

def _silu(x):
    return jax.nn.silu(x)

def _sigmoid(x):
    return jax.nn.sigmoid(x)

def _layernorm(x, axis=-1, eps=1e-05):
    m = jnp.mean(x, axis=axis, keepdims=True)
    v = jnp.var(x, axis=axis, keepdims=True)
    return (x - m) / jnp.sqrt(v + eps)

def _scatter_add(tgt, idx, src, axis=0):
    return tgt.at[idx].add(src)

def _segment_sum(src, seg, n):
    return jax.ops.segment_sum(src, seg, n)
kernel_name = 'mk_seq_preln_d2_jaxref_r4_fa5cc8'

def setup_inputs(seed: int=0):
    np.random.seed(seed)
    _w = jnp.asarray

    def _L0_attn_setup():
        import jax, jax.numpy as jnp
        import numpy as np
        HIDDEN = 256
        HEADS = 16
        HEAD_DIM = HIDDEN // HEADS
        BLOCK = 256
        B, S = (1, 1024)

        def _ring_attention(q, k, v, block, scale):
            b, h, s, d = q.shape
            nb = s // block
            kb = jnp.moveaxis(k.reshape(b, h, nb, block, d), 2, 0)
            vb = jnp.moveaxis(v.reshape(b, h, nb, block, d), 2, 0)

            def step(carry, kv):
                num, den = carry
                k_blk, v_blk = kv
                s_blk = jnp.einsum('bhqd,bhkd->bhqk', q, k_blk) * scale
                m = jnp.max(s_blk, axis=-1, keepdims=True)
                e = jnp.exp(s_blk - m)
                num = num + jnp.einsum('bhqk,bhkd->bhqd', e, v_blk)
                den = den + jnp.sum(e, axis=-1, keepdims=True)
                return ((num, den), None)
            init = (jnp.zeros_like(q), jnp.zeros((b, h, s, 1), dtype=q.dtype))
            (num, den), _ = jax.lax.scan(step, init, (kb, vb))
            return num / den
        key = jax.random.key(seed)
        k0, k1, k2, k3, k4 = jax.random.split(key, 5)
        w_scale = 0.02
        return {'hidden_states': jax.random.normal(k0, (B, S, HIDDEN), dtype=jnp.float32), 'w_q': jax.random.normal(k1, (HIDDEN, HIDDEN), dtype=jnp.float32) * w_scale, 'w_k': jax.random.normal(k2, (HIDDEN, HIDDEN), dtype=jnp.float32) * w_scale, 'w_v': jax.random.normal(k3, (HIDDEN, HIDDEN), dtype=jnp.float32) * w_scale, 'w_o': jax.random.normal(k4, (HIDDEN, HIDDEN), dtype=jnp.float32) * w_scale}
    _L0_attn_in = _L0_attn_setup()

    def _L0_ffn_setup():
        import jax, jax.numpy as jnp
        import numpy as np

        def _bitlinear(x, w_latent):
            scale = jax.lax.stop_gradient(jnp.clip(jnp.mean(jnp.abs(w_latent), axis=1, keepdims=True), 1e-05, None))
            tern = jnp.clip(jnp.round(w_latent / scale), -1.0, 1.0)
            w = w_latent + jax.lax.stop_gradient(tern - w_latent)
            return x @ (w * scale).T
        key = jax.random.key(seed)
        ks = jax.random.split(key, 6)
        dim, hidden, rank = (256, 1024, 16)
        B, S = (4, 1024)
        x = jax.random.normal(ks[0], (B, S, dim), dtype=jnp.float32)
        w_fc = 0.02 * jax.random.normal(ks[1], (hidden, dim), dtype=jnp.float32)
        w_proj = 0.02 * jax.random.normal(ks[2], (dim, hidden), dtype=jnp.float32)
        u = 0.02 * jax.random.normal(ks[3], (hidden, rank), dtype=jnp.float32)
        v = 0.02 * jax.random.normal(ks[4], (rank, dim), dtype=jnp.float32)
        fast_b = jax.random.normal(ks[5], (rank, rank), dtype=jnp.float32)
        gate = jnp.float32(0.05)
        return {'x': x, 'fast_b': fast_b, 'w_fc': w_fc, 'w_proj': w_proj, 'u': u, 'v': v, 'gate': gate}
    _L0_ffn_in = _L0_ffn_setup()

    def _L1_attn_setup():
        import jax, jax.numpy as jnp
        import numpy as np
        EMBED = 256
        HEADS = 16
        HEAD_DIM = EMBED // HEADS
        key = jax.random.key(seed)
        k1, k2, k3, k4, k5 = jax.random.split(key, 5)
        scale = 1.0 / np.sqrt(EMBED)
        return {'x': jax.random.normal(k1, (4, 512, EMBED), dtype=jnp.float32), 'qkv_w': jax.random.uniform(k2, (3 * EMBED, EMBED), minval=-scale, maxval=scale, dtype=jnp.float32), 'qkv_b': jax.random.uniform(k3, (3 * EMBED,), minval=-scale, maxval=scale, dtype=jnp.float32), 'out_w': jax.random.uniform(k4, (EMBED, EMBED), minval=-scale, maxval=scale, dtype=jnp.float32), 'out_b': jax.random.uniform(k5, (EMBED,), minval=-scale, maxval=scale, dtype=jnp.float32)}
    _L1_attn_in = _L1_attn_setup()

    def _L1_ffn_setup():
        import jax, jax.numpy as jnp
        import numpy as np
        DIM = 256
        DEPTH = 7
        PAR = 8
        N_NODES = 2 ** (DEPTH + 1) - 1
        WIDTH = PAR * N_NODES
        key = jax.random.key(seed)
        k1, k2, k3, k4 = jax.random.split(key, 4)
        init_k = float(np.sqrt(1.0 / DIM))
        init_k2 = float(np.sqrt(1.0 / ((DEPTH + 1) * PAR)))
        oldx = jax.random.normal(k1, (4, 512, DIM), dtype=jnp.float32)
        W_in = jax.random.uniform(k2, (WIDTH, DIM), jnp.float32, -init_k, init_k)
        b_in = jax.random.uniform(k3, (WIDTH,), jnp.float32, -init_k, init_k)
        W_out = jax.random.uniform(k4, (DIM, WIDTH), jnp.float32, -init_k2, init_k2)
        return {'oldx': oldx, 'W_in': W_in, 'b_in': b_in, 'W_out': W_out}
    _L1_ffn_in = _L1_ffn_setup()
    _d = {'L0_attn_hidden_states': _L0_attn_in['hidden_states'], 'L0_attn_w_q': _L0_attn_in['w_q'], 'L0_attn_w_k': _L0_attn_in['w_k'], 'L0_attn_w_v': _L0_attn_in['w_v'], 'L0_attn_w_o': _L0_attn_in['w_o'], 'L0_ffn_fast_b': _L0_ffn_in['fast_b'], 'L0_ffn_w_fc': _L0_ffn_in['w_fc'], 'L0_ffn_w_proj': _L0_ffn_in['w_proj'], 'L0_ffn_u': _L0_ffn_in['u'], 'L0_ffn_v': _L0_ffn_in['v'], 'L0_ffn_gate': _L0_ffn_in['gate'], 'L1_attn_qkv_w': _L1_attn_in['qkv_w'], 'L1_attn_qkv_b': _L1_attn_in['qkv_b'], 'L1_attn_out_w': _L1_attn_in['out_w'], 'L1_attn_out_b': _L1_attn_in['out_b'], 'L1_ffn_W_in': _L1_ffn_in['W_in'], 'L1_ffn_b_in': _L1_ffn_in['b_in'], 'L1_ffn_W_out': _L1_ffn_in['W_out']}
    _x0 = _d['L0_attn_hidden_states']
    _d['L0_attn_hidden_states'] = jax.random.normal(jax.random.fold_in(jax.random.key(seed), 1), (16, 512, 256), dtype=_x0.dtype)
    del _x0
    return _d

def reference(L0_attn_hidden_states, L0_attn_w_q, L0_attn_w_k, L0_attn_w_v, L0_attn_w_o, L0_ffn_fast_b, L0_ffn_w_fc, L0_ffn_w_proj, L0_ffn_u, L0_ffn_v, L0_ffn_gate, L1_attn_qkv_w, L1_attn_qkv_b, L1_attn_out_w, L1_attn_out_b, L1_ffn_W_in, L1_ffn_b_in, L1_ffn_W_out):

    def _L0_attn_ref(hidden_states, w_q, w_k, w_v, w_o):
        import jax, jax.numpy as jnp
        import numpy as np
        HIDDEN = 256
        HEADS = 16
        HEAD_DIM = HIDDEN // HEADS
        BLOCK = 256
        B, S = (1, 1024)

        def _ring_attention(q, k, v, block, scale):
            b, h, s, d = q.shape
            nb = s // block
            kb = jnp.moveaxis(k.reshape(b, h, nb, block, d), 2, 0)
            vb = jnp.moveaxis(v.reshape(b, h, nb, block, d), 2, 0)

            def step(carry, kv):
                num, den = carry
                k_blk, v_blk = kv
                s_blk = jnp.einsum('bhqd,bhkd->bhqk', q, k_blk) * scale
                m = jnp.max(s_blk, axis=-1, keepdims=True)
                e = jnp.exp(s_blk - m)
                num = num + jnp.einsum('bhqk,bhkd->bhqd', e, v_blk)
                den = den + jnp.sum(e, axis=-1, keepdims=True)
                return ((num, den), None)
            init = (jnp.zeros_like(q), jnp.zeros((b, h, s, 1), dtype=q.dtype))
            (num, den), _ = jax.lax.scan(step, init, (kb, vb))
            return num / den
        b, s, _ = hidden_states.shape
        q = (hidden_states @ w_q).reshape(b, s, HEADS, HEAD_DIM).transpose(0, 2, 1, 3)
        k = (hidden_states @ w_k).reshape(b, s, HEADS, HEAD_DIM).transpose(0, 2, 1, 3)
        v = (hidden_states @ w_v).reshape(b, s, HEADS, HEAD_DIM).transpose(0, 2, 1, 3)
        scale = HEAD_DIM ** (-0.5)
        out = _ring_attention(q, k, v, BLOCK, scale)
        out = out.transpose(0, 2, 1, 3).reshape(b, s, HIDDEN)
        return out @ w_o

    def _L0_ffn_ref(x, fast_b, w_fc, w_proj, u, v, gate):
        import jax, jax.numpy as jnp
        import numpy as np

        def _bitlinear(x, w_latent):
            scale = jax.lax.stop_gradient(jnp.clip(jnp.mean(jnp.abs(w_latent), axis=1, keepdims=True), 1e-05, None))
            tern = jnp.clip(jnp.round(w_latent / scale), -1.0, 1.0)
            w = w_latent + jax.lax.stop_gradient(tern - w_latent)
            return x @ (w * scale).T
        h = _bitlinear(x, w_fc) + gate * (x @ v.T @ fast_b.T @ u.T)
        r = jnp.maximum(h, 0.0)
        return _bitlinear(r * r, w_proj)

    def _L1_attn_ref(x, qkv_w, qkv_b, out_w, out_b):
        import jax, jax.numpy as jnp
        import numpy as np
        EMBED = 256
        HEADS = 16
        HEAD_DIM = EMBED // HEADS
        b, n, _ = x.shape
        qkv = (jnp.einsum('bne,fe->bnf', x, qkv_w) + qkv_b).reshape(b, n, 3, HEADS, HEAD_DIM)
        q, k, v = (qkv[:, :, 0], qkv[:, :, 1], qkv[:, :, 2])
        scores = jnp.einsum('bnhd,bmhd->bhnm', q, k) / jnp.sqrt(jnp.float32(HEAD_DIM))
        attn = jax.nn.softmax(scores, axis=-1)
        out = jnp.einsum('bhnm,bmhd->bnhd', attn, v).reshape(b, n, EMBED)
        return jnp.einsum('bne,fe->bnf', out, out_w) + out_b

    def _L1_ffn_ref(oldx, W_in, b_in, W_out):
        import jax, jax.numpy as jnp
        import numpy as np
        DIM = 256
        DEPTH = 7
        PAR = 8
        N_NODES = 2 ** (DEPTH + 1) - 1
        WIDTH = PAR * N_NODES
        x = oldx.reshape(-1, DIM)
        B = x.shape[0]
        logits = x @ W_in.T + b_in
        decisions = (logits > 0).astype(jnp.int32).reshape(B, PAR, N_NODES)
        acts = jax.nn.silu(logits).reshape(B, PAR, N_NODES)
        current = jnp.zeros((B, PAR), dtype=jnp.int32)
        dmap = jax.nn.one_hot(current, N_NODES, dtype=acts.dtype)
        for d in range(DEPTH):
            cur_platform = 2 ** d - 1
            next_platform = 2 ** (d + 1) - 1
            moves = jnp.take_along_axis(decisions, current[..., None], axis=2)[..., 0]
            current = (current - cur_platform) * 2 + moves + next_platform
            dmap = dmap + jax.nn.one_hot(current, N_NODES, dtype=acts.dtype)
        masked = acts * jax.lax.stop_gradient(dmap)
        out = masked.reshape(B, WIDTH) @ W_out.T
        return out.reshape(oldx.shape)
    x = L0_attn_hidden_states
    x = x + _L0_attn_ref(_layernorm(x, axis=-1), L0_attn_w_q, L0_attn_w_k, L0_attn_w_v, L0_attn_w_o)
    x = x + _L0_ffn_ref(_layernorm(x, axis=-1), L0_ffn_fast_b, L0_ffn_w_fc, L0_ffn_w_proj, L0_ffn_u, L0_ffn_v, L0_ffn_gate)
    x = x + _L1_attn_ref(_layernorm(x, axis=-1), L1_attn_qkv_w, L1_attn_qkv_b, L1_attn_out_w, L1_attn_out_b)
    x = x + _L1_ffn_ref(_layernorm(x, axis=-1), L1_ffn_W_in, L1_ffn_b_in, L1_ffn_W_out)
    return x

_drawn_inputs = setup_inputs


def setup_inputs(seed=0):
    import zlib

    import numpy as np

    out = dict(_drawn_inputs(seed))
    spreads = {}
    factors = {'L0_attn_w_q': 8.0,
     'L0_attn_w_k': 8.0,
     'L0_attn_w_v': 3.416,
     'L0_attn_w_o': 3.425,
     'L0_ffn_fast_b': 8.0,
     'L0_ffn_u': 8.0,
     'L0_ffn_v': 8.0,
     'L1_attn_qkv_b': 8.0,
     'L1_attn_out_b': 8.0,
     'L1_ffn_b_in': 6.837}
    for name, (base, spread) in spreads.items():
        noise = np.random.default_rng([zlib.crc32(name.encode()), seed]).standard_normal(out[name].shape)
        drawn = base * np.exp(spread * noise) if base else spread * noise
        out[name] = jnp.asarray(drawn.astype(out[name].dtype))
    for name, factor in factors.items():
        out[name] = (out[name] * factor).astype(out[name].dtype)
    return out
```

```python
import concourse.bass as bass
from concourse import mybir
from contextlib import ExitStack
import numpy as np

F32 = mybir.dt.float32
BF16 = mybir.dt.bfloat16
ACT = mybir.ActivationFunctionType
ALU = mybir.AluOpType
AX = mybir.AxisListType

P = 128
B, S, D = 16, 512, 256
T = S // P
KD = D // P
H = 16
HD = D // H
HH = P // HD
G = 4
NG = H // G
QSCALE = HD ** -0.5
BLK = 256
F0 = 1024
M0 = F0 // P
PAR, DEPTH = 8, 7
NODES = 2 ** (DEPTH + 1) - 1
INNER = 2 ** DEPTH - 1
LEAVES = NODES - INNER
EPS = 1e-5
RANK = 16

QPART = [0, 0, 1, 0, 2, 1]
KPART = [0, 1, 0, 2, 0, 1]
SLOTS = len(QPART)
MROW = SLOTS * HD
NMR = 3 * (S // BLK)
KROWS = MROW + NMR
LEAD = 5


def build(nc, t, out):
    ctx = ExitStack()
    with ctx:
        def sb(name, shape, dt=F32):
            return ctx.enter_context(nc.sbuf_tensor(name, shape, dt))

        def sem(name):
            return ctx.enter_context(nc.semaphore(name))

        xin = sb("xin", [P, T, D])
        x = sb("x", [P, T, D])
        h = sb("h", [P, T, D])
        hT = sb("hT", [P, KD, S])
        wq = [sb(f"wq{l}", [P, KD, D]) for l in range(2)]
        wk = [sb(f"wk{l}", [P, KD, D]) for l in range(2)]
        wv = [sb(f"wv{l}", [P, KD, D]) for l in range(2)]
        wo = [sb(f"wo{l}", [P, KD, D]) for l in range(2)]
        wfc = sb("wfc", [P, KD, F0])
        wpr = sb("wpr", [P, M0, D])
        win = sb("win", [P, KD, PAR, NODES])
        wout = sb("wout", [P, PAR, 2, D])
        bqk = sb("bqk", [P, 4])
        bv = sb("bv", [P, 2, D])
        bo = sb("bo", [P, D])
        bin_ = sb("bin_", [P, PAR, 2])
        anc = sb("anc", [INNER, NODES], BF16)
        thr = sb("thr", [P, 2])
        idf = sb("idf", [P, P])
        idb = sb("idb", [P, P], BF16)
        gate = sb("gate", [P, 1])
        qst = sb("qst", [KROWS, H, S], BF16)
        kst = sb("kst", [KROWS, H, S], BF16)
        qk = sb("qk", [P, 4, S])
        parts = sb("parts", [P, 3, 4, S], BF16)
        y = parts[:, 0, :, :].bitcast(F32)
        vn = sb("vn", [P, T, H, 2 * HD])
        probs = sb("probs", [P, 2, T, G, S])
        oT = qk
        nmax = sb("nmax", [P, 2, T, 2, 2])
        nres = sb("nres", [P, 2, T, 2, 2])
        npart = sb("npart", [P, 2, T, 3, 2, 2], BF16)
        nrow = sb("nrow", [2 * NMR, 2, S], BF16)
        rden = sb("rden", [P, T, H])
        stats = sb("stats", [P, T, 6])
        mean = sb("mean", [P, T])
        dif = sb("dif", [P, T])
        vpe = sb("vpe", [P, T])
        rstd = sb("rstd", [P, T])
        mhalf = sb("mhalf", [P, T])
        zero = sb("zero", [P, T, 2, 2])

        pr = probs[:].rearrange("p a b c s -> p (a b c) s")
        r2 = pr[:, 0:M0, :]
        rr = pr[:, M0:M0 + 4, :]
        actv = pr[:, 0:4, :].rearrange("p (a b) s -> p a b s", a=2)
        masked = pr[:, 4:8, :].rearrange("p (a b) s -> p a b s", a=2)
        dec = pr[:, 8:9, :].bitcast(BF16).rearrange("p o (a s) -> p (o a) s", a=2)
        wabs = pr[:, 0:4, :].rearrange("p a s -> p (a s)")
        tgt = pr[:, 4:8, :].rearrange("p a s -> p (a s)")
        tlt = pr[:, 8:12, :].rearrange("p a s -> p (a s)")
        scl = pr[:, 12:14, :].rearrange("p a s -> p (a s)")
        hlf = pr[:, 14:16, :].rearrange("p a s -> p (a s)")
        nhl = pr[:, 16:18, :].rearrange("p a s -> p (a s)")
        fbs = pr[0:RANK, 18:19, 0:RANK].rearrange("p a s -> p (a s)")
        uTs = pr[0:RANK, 19:21, :].rearrange("p a s -> p (a s)")
        vs = pr[0:RANK, 21:22, 0:D].rearrange("p a s -> p (a s)")
        g1 = pr[0:RANK, 22:24, :].rearrange("p a s -> p (a s)")
        onesf = pr[:, 24:25, 0:P].rearrange("p a s -> p (a s)")
        onesp = pr[:, 24:25, P:2 * P].rearrange("p a s -> p (a s)")

        ps = ctx.enter_context(nc.psum_tensor("ps", [P, 8, S], F32))
        bank = [ps[:, i, :] for i in range(8)]
        mrow_bank = bank[7].bitcast(BF16)

        w_in = sem("w_in")
        abs_done = sem("abs_done")
        mean_ps = sem("mean_ps")
        tern = sem("tern")
        g1_ps = sem("g1_ps")
        g1_sb = sem("g1_sb")
        low_ps = sem("low_ps")
        ones_set = sem("ones_set")
        pool_set = sem("pool_set")
        x_in = sem("x_in")
        ln_stats = sem("ln_stats")
        ln_mv = sem("ln_mv")
        ln_rstd = sem("ln_rstd")
        ln_h = sem("ln_h")
        hT_ps = sem("hT_ps")
        hT_act = sem("hT_act")
        hT_dve = sem("hT_dve")
        xb_done = sem("xb_done")
        qk_ps = sem("qk_ps")
        v_ps = sem("v_ps")
        qk_sb = sem("qk_sb")
        split = sem("split")
        v_sb = sem("v_sb")
        stack = [sem("stack0"), sem("stack1")]
        max_ps = sem("max_ps")
        max_rd = sem("max_rd")
        msplit = sem("msplit")
        mrow_ps = sem("mrow_ps")
        mrow_sb = sem("mrow_sb")
        mstack = [sem("mstack0"), sem("mstack1")]
        exp_ps = sem("exp_ps")
        exp_rd = sem("exp_rd")
        pv_step = sem("pv_step")
        oT_sb = sem("oT_sb")
        nat_ps = sem("nat_ps")
        rden_sb = sem("rden_sb")
        attn_sb = sem("attn_sb")
        aT_ps = sem("aT_ps")
        aT_act = sem("aT_act")
        aT_dve = sem("aT_dve")
        res_ps = sem("res_ps")
        x_upd = sem("x_upd")
        fc_ps = sem("fc_ps")
        relu_rd = sem("relu_rd")
        sq = sem("sq")
        lg_ps = sem("lg_ps")
        fc_used = sem("fc_used")
        lg_act = sem("lg_act")
        dec_sb = sem("dec_sb")
        sel_ps = sem("sel_ps")
        masked_sb = sem("masked_sb")
        y_sb = sem("y_sb")
        y_out = sem("y_out")

        block = ctx.enter_context(nc.Block())

        loads = [
            (wfc[:], t["wfcT"].rearrange("(k p) n -> p k n", p=P)),
            (wpr[:], t["wprT"].rearrange("(k p) n -> p k n", p=P)),
            (fbs, t["fast_b"]), (uTs, t["uT"]), (vs, t["v"]), (gate[:], t["gate"]),
            (idf[:], t["idf"]), (idb[:], t["idb"].bitcast(BF16)),
            (wq[0][:], t["wq0"].rearrange("(k p) n -> p k n", p=P)),
            (wk[0][:], t["wk0"].rearrange("(k p) n -> p k n", p=P)),
            (wv[0][:], t["wv0"].rearrange("(k p) n -> p k n", p=P)),
            (wo[0][:], t["wo0"].rearrange("(k p) n -> p k n", p=P)),
            (wq[1][:], t["wqkvT"][:, 0:D].rearrange("(k p) n -> p k n", p=P)),
            (wk[1][:], t["wqkvT"][:, D:2 * D].rearrange("(k p) n -> p k n", p=P)),
            (wv[1][:], t["wqkvT"][:, 2 * D:3 * D].rearrange("(k p) n -> p k n", p=P)),
            (wo[1][:], t["wo1T"].rearrange("(k p) n -> p k n", p=P)),
            (win[:].rearrange("p k a n -> p k (a n)"), t["winT"].rearrange("(k p) n -> p k n", p=P)),
            (wout[0:INNER, :, 0, :], t["woutT"].rearrange("(a n) e -> n a e", n=NODES)[0:INNER]),
            (wout[0:LEAVES, :, 1, :], t["woutT"].rearrange("(a n) e -> n a e", n=NODES)[INNER:NODES]),
            (bqk[:], t["bqk"]), (bv[:], t["bv"].rearrange("p (a n) -> p a n", a=2)),
            (bo[:], t["bo"]),
            (bin_[:], t["bin"].rearrange("p (a n) -> p a n", n=2)),
            (anc[:], t["anc"].bitcast(BF16)), (thr[:], t["thr"]),
            (kst[MROW:KROWS, :, :], t["krows"].bitcast(BF16).rearrange("r (a s) -> r a s", a=H)),
        ]
        ALL_IN = 16 * (len(loads) - 1)

        @block.sync
        def _(sp):
            for dst, src in loads[:-1]:
                sp.dma_start(dst, src).then_inc(w_in, 16)
            sp.dma_start(*loads[-1]).then_inc(y_out, 16)
            with sp.Fori(0, B) as b:
                sp.wait_ge(x_upd, 12 * b + 1)
                sp.dma_start(xin[:], t["x"][bass.ds(b, 1)].rearrange("o (t p) d -> p (o t) d", p=P)).then_inc(x_in, 16)
                for l in range(2):
                    n = b * 2 + l
                    for hf in range(2):
                        for part in range(3):
                            sp.wait_ge(split, n * 8 + (4 * hf + [1, 3, 4][part]))
                            for c, (dst, slots) in enumerate(((qst, QPART), (kst, KPART))):
                                for s in range(SLOTS):
                                    if slots[s] == part:
                                        sp.dma_start(
                                            dst[s * HD:(s + 1) * HD, hf * HH:(hf + 1) * HH, :],
                                            parts[:, part, 2 * hf + c, :],
                                        ).then_inc(stack[hf], 16)
                    for p in range(H // 2):
                        sp.wait_ge(mrow_sb, n * (H // 2) + (p + 1))
                        sp.dma_start(qst[MROW:KROWS, 2 * p:2 * p + 2, :],
                                     nrow[:, p % 2, :]).then_inc(mstack[p % 2], 16)

        @block.gpsimd
        def _(pool):
            nc.gpsimd.memset(mhalf[:], -0.5).then_inc(pool_set, 1)
            nc.gpsimd.memset(zero[:], 0.0).then_inc(pool_set, 1)
            pool.wait_ge(pool_set, 2)

            def rstd_of(m):
                pool.wait_ge(ln_mv, m * 7 + 7)
                nc.gpsimd.tensor_tensor(rstd[:], vpe[:], mhalf[:], ALU.pow).then_inc(ln_rstd, 1)

            with pool.Fori(0, B) as b:
                for l in range(2):
                    n = b * 2 + l
                    rstd_of(b * 4 + 2 * l)
                    if l == 1:
                        pool.wait_ge(w_in, ALL_IN)
                        pool.wait_ge(ln_h, b * 4 * T + 3 * T)
                        nc.gpsimd.tensor_tensor(x[:], x[:], bo[:].rearrange("p (o d) -> p o d", o=1).to_broadcast([P, T, D]), ALU.add).then_inc(xb_done, 1)
                    for p in range(H // 2):
                        u = p % 2
                        pool.wait_ge(max_rd, n * (H * T) + (p + 1) * 2 * T)
                        if p >= 2:
                            pool.wait_ge(mrow_ps, n * (H // 2) + (p - 1))
                        a = nmax[:, u, :, :, :] if l == 0 else nmax[:, u, :, 0:1, :].to_broadcast([P, T, 2, 2])
                        q = npart[:, u, :, :, :, :]
                        k = n * (4 * (H // 2)) + 4 * p
                        nc.gpsimd.tensor_tensor(q[:, :, 0, :, :], a, zero[:], ALU.add).then_inc(msplit, 1)
                        pool.wait_ge(msplit, k + 1)
                        nc.gpsimd.tensor_tensor(nres[:, u], a, q[:, :, 0, :, :], ALU.subtract).then_inc(msplit, 1)
                        pool.wait_ge(msplit, k + 2)
                        nc.gpsimd.tensor_tensor(q[:, :, 1, :, :], nres[:, u], zero[:], ALU.add).then_inc(msplit, 1)
                        pool.wait_ge(msplit, k + 3)
                        nc.gpsimd.tensor_tensor(q[:, :, 2, :, :], nres[:, u], q[:, :, 1, :, :], ALU.subtract).then_inc(msplit, 1)
                    rstd_of(b * 4 + 2 * l + 1)
                    if l == 0:
                        for m in range(M0):
                            pool.wait_ge(relu_rd, b * M0 + (m + 1))
                            nc.gpsimd.tensor_tensor(r2[:, m, :], rr[:, m % 4, :], rr[:, m % 4, :], ALU.mult).then_inc(sq, 1)

        @block.scalar
        def _(act):
            act.wait_ge(w_in, ALL_IN)
            nc.scalar.activation(wabs, wfc[:].rearrange("p k n -> p (k n)"), ACT.Abs).then_inc(abs_done, 1)
            act.wait_ge(mean_ps, 2)
            nc.scalar.activation(wabs, wpr[:].rearrange("p k n -> p (k n)"), ACT.Abs).then_inc(abs_done, 1)
            act.wait_ge(g1_ps, 2)
            nc.scalar.activation(g1, ps[0:RANK, 4:6, :].rearrange("p a s -> p (a s)"), ACT.Copy).then_inc(g1_sb, 1)

            def hT_copy(m):
                act.wait_ge(hT_ps, m * KD + 1)
                nc.scalar.activation(hT[:, 0, :], bank[0], ACT.Copy).then_inc(hT_act, 1)

            with act.Fori(0, B) as b:
                for l in range(2):
                    n = b * 2 + l
                    hT_copy(b * 4 + 2 * l)
                    for c in range(4):
                        act.wait_ge(qk_ps, n * 4 + (c + 1))
                        nc.scalar.activation(qk[:, c, :], bank[2 + c], ACT.Identity, scale=1.0 if c % 2 else QSCALE,
                                             bias=bqk[:, c:c + 1] if l else 0.0).then_inc(qk_sb, 1)
                    for s in range(-2, H + G + 1):
                        for hf in range(2):
                            if hf == 1:
                                if s % 2 == 0 and (s + 2) // 2 < H // 2:
                                    p = (s + 2) // 2
                                    act.wait_ge(mrow_ps, n * (H // 2) + (p + 1))
                                    if p >= 2:
                                        act.wait_ge(mstack[p % 2], n * (4 * 16) + 16 * (p // 2))
                                    nc.scalar.activation(nrow[:, p % 2, :], mrow_bank[0:2 * NMR, 0:S], ACT.Copy).then_inc(mrow_sb, 1)
                                if s % G == 0 and s >= 2 * G:
                                    g = s // G - 2
                                    act.wait_ge(pv_step, n * (4 * NG) + 4 * (g + 1))
                                    nc.scalar.activation(oT[:, g, :], bank[6], ACT.Copy).then_inc(oT_sb, 1)
                            if 0 <= s < H:
                                g = s // G
                                if s % G == 0 and hf == 0 and g >= 2:
                                    act.wait_ge(pv_step, n * (4 * NG) + 4 * (g - 1))
                                act.wait_ge(exp_ps, n * (2 * H) + (2 * s + hf + 1))
                                nc.scalar.activation(probs[:, g % 2, 2 * hf:2 * hf + 2, s % G, :],
                                                     ps[:, 2 + 2 * hf:4 + 2 * hf, :], ACT.Exp).then_inc(exp_rd, 1)
                    act.wait_ge(aT_ps, n * KD + 1)
                    nc.scalar.activation(hT[:, 0, :], bank[0], ACT.Copy).then_inc(aT_act, 1)
                    hT_copy(b * 4 + 2 * l + 1)
                    if l == 0:
                        for m in range(M0):
                            act.wait_ge(fc_ps, b * M0 + (m + 1))
                            if m >= 4:
                                act.wait_ge(sq, b * M0 + (m - 3))
                            nc.scalar.activation(rr[:, m % 4, :], bank[[2, 3, 0, 1][m % 4]], ACT.Relu).then_inc(relu_rd, 1)
                    else:
                        for a in range(PAR):
                            for leaf, rows in ((1, LEAVES), (0, INNER)):
                                if leaf:
                                    act.wait_ge(lg_ps, b * (2 * PAR) + (2 * a + 2))
                                    if a >= 2:
                                        act.wait_ge(masked_sb, b * (2 * PAR) + 2 * (a - 1))
                                else:
                                    act.wait_ge(dec_sb, b * PAR + (a + 1))
                                nc.scalar.activation(actv[0:rows, a % 2, leaf, :], bank[leaf][0:rows], ACT.Silu,
                                                     bias=bin_[0:rows, a, leaf:leaf + 1]).then_inc(lg_act, 1)
                act.wait_ge(y_sb, b * T + T)
                act.dma_start(out[bass.ds(b, 1)].rearrange("o (t p) d -> p (o t) d", p=P), y).then_inc(y_out, 16)
            act.wait_ge(y_out, 16 * B + 16)

        @block.vector
        def _(dve):
            dve.wait_ge(w_in, ALL_IN)
            nc.vector.memset(onesf, 1.0 / D).then_inc(ones_set, 1)
            nc.vector.memset(onesp, 1.0 / F0).then_inc(ones_set, 1)
            nc.vector.memset(vn[:], 1.0).then_inc(ones_set, 1)
            nc.vector.memset(xin[:, 0, 0:1], 0.0).then_inc(x_upd, 1)
            nc.vector.tensor_scalar_mul(bqk[:, 0:4:2], bqk[:, 0:4:2], QSCALE).then_inc(ones_set, 1)
            step = 0

            def bitlinear(w, K, N, src, seen):
                nonlocal step
                wf = w[:]
                v3 = lambda a: a[:, 0:K * N].rearrange("p (k n) -> p k n", k=K)
                bc = lambda a: a[:, 0:N].rearrange("p (o n) -> p o n", o=1).to_broadcast([P, K, N])
                dve.wait_ge(mean_ps, seen)
                for ins in (
                    lambda: nc.vector.tensor_scalar_max(scl[:, 0:N], src, 1e-5),
                    lambda: nc.vector.tensor_scalar_mul(hlf[:, 0:N], scl[:, 0:N], 0.5),
                    lambda: nc.vector.tensor_scalar_mul(nhl[:, 0:N], scl[:, 0:N], -0.5),
                    lambda: nc.vector.tensor_tensor(v3(tgt), wf, bc(hlf), ALU.is_gt),
                    lambda: nc.vector.tensor_tensor(v3(tlt), wf, bc(nhl), ALU.is_lt),
                    lambda: nc.vector.tensor_tensor(v3(tgt), v3(tgt), v3(tlt), ALU.subtract),
                    lambda: nc.vector.tensor_tensor(v3(tgt), v3(tgt), wf, ALU.subtract),
                    lambda: nc.vector.tensor_tensor(wf, wf, v3(tgt), ALU.add),
                    lambda: nc.vector.tensor_tensor(wf, wf, bc(scl), ALU.mult),
                ):
                    ins().then_inc(tern, 1)
                    step += 1
                    dve.wait_ge(tern, step)

            bitlinear(wfc, KD, F0, ps[:, 0:2, :].rearrange("p a s -> p (a s)"), 2)
            bitlinear(wpr, M0, D, bank[2][:, 0:D], 3)
            for k in range(KD):
                dve.wait_ge(low_ps, 2 * (k + 1))
                nc.vector.scalar_tensor_tensor(
                    wfc[:, k, :], ps[:, [0, 6][k]:[0, 6][k] + 2, :].rearrange("p a s -> p (a s)"), gate[:, 0:1],
                    wfc[:, k, :], ALU.mult, ALU.add).then_inc(tern, 1)
                step += 1
            dve.wait_ge(tern, step)

            def layernorm(b, i, src):
                m = b * 4 + i
                for tt in range(T):
                    nc.vector.bn_stats(stats[:, tt, :], src[:, tt, :]).then_inc(ln_stats, 1)
                even, odd = stats[:, :, 0:3], stats[:, :, 3:6]
                dve.wait_ge(ln_stats, m * T + T)
                nc.vector.tensor_tensor(mean[:], even[:, :, 1], odd[:, :, 1], ALU.add).then_inc(ln_mv, 1)
                nc.vector.tensor_tensor(dif[:], even[:, :, 1], odd[:, :, 1], ALU.subtract).then_inc(ln_mv, 1)
                nc.vector.tensor_tensor(vpe[:], even[:, :, 2], odd[:, :, 2], ALU.add).then_inc(ln_mv, 1)
                dve.wait_ge(ln_mv, m * 7 + 3)
                nc.vector.tensor_scalar(mean[:], mean[:], 0.5, None, ALU.mult).then_inc(ln_mv, 1)
                nc.vector.tensor_tensor(dif[:], dif[:], dif[:], ALU.mult).then_inc(ln_mv, 1)
                nc.vector.tensor_scalar(vpe[:], vpe[:], 1.0 / D, EPS, ALU.mult, ALU.add).then_inc(ln_mv, 1)
                dve.wait_ge(ln_mv, m * 7 + 6)
                nc.vector.scalar_tensor_tensor(vpe[:], dif[:], 0.25, vpe[:], ALU.mult, ALU.add).then_inc(ln_mv, 1)
                dve.wait_ge(ln_rstd, m + 1)
                for tt in range(T):
                    nc.vector.tensor_scalar(h[:, tt, :], src[:, tt, :], mean[:, tt:tt + 1], rstd[:, tt:tt + 1],
                                            ALU.subtract, ALU.mult).then_inc(ln_h, 1)
                dve.wait_ge(hT_ps, m * KD + KD)
                nc.vector.tensor_copy(hT[:, 1, :], bank[1]).then_inc(hT_dve, 1)

            with dve.Fori(0, B) as b:
                for l in range(2):
                    n = b * 2 + l
                    if l == 0:
                        dve.wait_ge(x_in, b * 16 + 16)
                    src = xin if l == 0 else x
                    layernorm(b, 2 * l, src)
                    dve.wait_ge(y_out, b * 16 + 16)
                    for hf in range(2):
                        dve.wait_ge(qk_sb, n * 4 + 2 * (hf + 1))
                        c = slice(2 * hf, 2 * hf + 2)
                        nc.vector.tensor_copy(parts[:, 0, c, :], qk[:, c, :]).then_inc(split, 1)
                        dve.wait_ge(split, n * 8 + (4 * hf + 1))
                        nc.vector.tensor_tensor(qk[:, c, :], qk[:, c, :], parts[:, 0, c, :], ALU.subtract).then_inc(split, 1)
                        dve.wait_ge(split, n * 8 + (4 * hf + 2))
                        nc.vector.tensor_copy(parts[:, 1, c, :], qk[:, c, :]).then_inc(split, 1)
                        dve.wait_ge(split, n * 8 + (4 * hf + 3))
                        nc.vector.tensor_tensor(parts[:, 2, c, :], qk[:, c, :], parts[:, 1, c, :], ALU.subtract).then_inc(split, 1)
                    for u in range(2):
                        dve.wait_ge(v_ps, n * 2 + (u + 1))
                        dst = vn[:, 2 * u:2 * u + 2, :, 0:HD]
                        sv = bank[6 + u].rearrange("p (t a d) -> p t a d", t=2, d=HD)
                        if l == 0:
                            nc.vector.tensor_copy(dst, sv).then_inc(v_sb, 1)
                        else:
                            nc.vector.tensor_tensor(dst, sv, bv[:].rearrange("p t (a d) -> p t a d", d=HD), ALU.add).then_inc(v_sb, 1)
                    for e in range(H):
                        p = e // 2
                        if e % 2 == 0 and p >= 2:
                            dve.wait_ge(msplit, n * (4 * (H // 2)) + 4 * (p - 1))
                        for tt in range(T):
                            dve.wait_ge(max_ps, n * (H * T) + (T * e + tt + 1))
                            src_ps = bank[tt % 2]
                            if l == 0:
                                nc.vector.tensor_reduce(nmax[:, p % 2, tt, :, e % 2], src_ps.rearrange("p (a s) -> p a s", s=BLK),
                                                        AX.X, ALU.max, negate=True).then_inc(max_rd, 1)
                            else:
                                nc.vector.tensor_reduce(nmax[:, p % 2, tt, 0, e % 2:e % 2 + 1], src_ps,
                                                        AX.X, ALU.max, negate=True).then_inc(max_rd, 1)
                    for tt in range(T):
                        nat = bank[2 + tt].rearrange("p (a c) -> p a c", c=2 * HD)
                        dve.wait_ge(nat_ps, n * T + (tt + 1))
                        nc.vector.reciprocal(rden[:, tt, :], nat[:, :, HD]).then_inc(rden_sb, 1)
                        dve.wait_ge(rden_sb, n * T + (tt + 1))
                        nc.vector.tensor_tensor(h[:, tt, :].rearrange("p (a d) -> p a d", d=HD), nat[:, :, 0:HD],
                                                rden[:, tt, :].rearrange("p (a o) -> p a o", o=1).to_broadcast([P, H, HD]),
                                                ALU.mult).then_inc(attn_sb, 1)
                    dve.wait_ge(aT_ps, n * KD + KD)
                    nc.vector.tensor_copy(hT[:, 1, :], bank[1]).then_inc(aT_dve, 1)
                    if l == 1:
                        dve.wait_ge(xb_done, b + 1)
                    for tt in range(T):
                        dve.wait_ge(res_ps, b * (4 * T) + (2 * l * T + tt + 1))
                        nc.vector.tensor_tensor(x[:, tt, :], bank[2 + tt][:, 0:D], src[:, tt, :], ALU.add).then_inc(x_upd, 1)
                    dve.wait_ge(x_upd, b * 12 + (8 * l + T + 1))
                    layernorm(b, 2 * l + 1, x)
                    if l == 0:
                        for tt in range(T):
                            dve.wait_ge(res_ps, b * (4 * T) + (T + tt + 1))
                            nc.vector.tensor_tensor(x[:, tt, :], bank[4 + tt][:, 0:D], x[:, tt, :], ALU.add).then_inc(x_upd, 1)
                        dve.wait_ge(x_upd, b * 12 + 9)
                    else:
                        for a in range(PAR + 1):
                            if a < PAR:
                                dve.wait_ge(lg_ps, b * (2 * PAR) + (2 * a + 1))
                                if a >= 2:
                                    dve.wait_ge(sel_ps, b * (2 * PAR) + 2 * (a - 1))
                                nc.vector.tensor_scalar(dec[0:INNER, a % 2, :], bank[0][0:INNER], bin_[0:INNER, a, 0:1], 0.0,
                                                        ALU.add, ALU.is_gt).then_inc(dec_sb, 1)
                            if a >= 1:
                                c = a - 1
                                for leaf, rows in ((0, INNER), (1, LEAVES)):
                                    dve.wait_ge(sel_ps, b * (2 * PAR) + (2 * c + leaf + 1))
                                    dve.wait_ge(lg_act, b * (2 * PAR) + (2 * c + 2))
                                    if c >= 2:
                                        dve.wait_ge(fc_used, b * (2 * PAR - 1) + (2 * (c - 2) + leaf + 1))
                                    nc.vector.scalar_tensor_tensor(
                                        masked[0:rows, c % 2, leaf, :], bank[2 + leaf][0:rows], thr[0:rows, leaf:leaf + 1],
                                        actv[0:rows, c % 2, leaf, :], ALU.is_equal, ALU.mult).then_inc(masked_sb, 1)
                        dve.wait_ge(y_out, b * 16 + 16)
                        for tt in range(T):
                            dve.wait_ge(res_ps, b * (4 * T) + (3 * T + tt + 1))
                            nc.vector.tensor_tensor(y[:, tt, :], bank[4 + tt][:, 0:D], x[:, tt, :], ALU.add).then_inc(y_sb, 1)

        @block.tensor
        def _(pe):
            mm = nc.tensor.matmul
            pe.wait_ge(w_in, ALL_IN)
            pe.wait_ge(ones_set, 4)
            pe.wait_ge(abs_done, 1)
            for j in range(2):
                for k in range(KD):
                    i = mm(bank[j], onesf, wabs[:, k * F0 + j * S:k * F0 + (j + 1) * S], start=k == 0, stop=k == KD - 1)
                i.then_inc(mean_ps, 1)
            pe.wait_ge(abs_done, 2)
            for k in range(M0):
                i = mm(bank[2][:, 0:D], onesp, wabs[:, k * D:(k + 1) * D], start=k == 0, stop=k == M0 - 1)
            i.then_inc(mean_ps, 1)
            for j in range(2):
                mm(bank[4 + j][0:RANK], fbs, uTs[:, j * S:(j + 1) * S], start=True, stop=True).then_inc(g1_ps, 1)
            pe.wait_ge(g1_sb, 1)
            pe.wait_ge(tern, 1)
            for k in range(KD):
                for j in range(2):
                    mm(bank[[0, 6][k] + j], vs[:, k * P:(k + 1) * P], g1[:, j * S:(j + 1) * S],
                       start=True, stop=True).then_inc(low_ps, 1)
            pe.wait_ge(tern, 20)
            pe.wait_ge(y_out, 16)

            def transposed(b, i):
                m = b * 4 + i
                for k in range(KD):
                    for tt in range(T):
                        if k == 0:
                            pe.wait_ge(ln_h, m * T + (tt + 1))
                        ins = nc.tensor.transpose(bank[k][:, tt * P:(tt + 1) * P], h[:, tt, k * P:(k + 1) * P], idf[:])
                    ins.then_inc(hT_ps, 1)
                pe.wait_ge(hT_act, m + 1)
                pe.wait_ge(hT_dve, m + 1)

            with pe.Fori(0, B) as b:
                for l in range(2):
                    n = b * 2 + l
                    transposed(b, 2 * l)
                    for hf in range(2):
                        for c, w in enumerate((wq[l], wk[l])):
                            for k in range(KD):
                                i = mm(bank[2 + 2 * hf + c], w[:, k, hf * P:(hf + 1) * P], hT[:, k, :], start=k == 0, stop=k == KD - 1)
                            i.then_inc(qk_ps, 1)
                    for tt in range(T):
                        for k in range(KD):
                            i = mm(bank[6 + tt // 2][:, tt % 2 * D:(tt % 2 + 1) * D], hT[:, k, tt * P:(tt + 1) * P],
                                   wv[l][:, k, :], start=k == 0, stop=k == KD - 1)
                        if tt % 2:
                            i.then_inc(v_ps, 1)
                    pe.wait_ge(qk_sb, n * 4 + 4)
                    for s in range(-LEAD, H + G):
                        e = s + LEAD
                        if e < H:
                            if e % HH == 0:
                                pe.wait_ge(stack[e // HH], n * (16 * 2 * SLOTS) + 16 * 2 * SLOTS)
                            for tt in range(T):
                                v = T * e + tt
                                if v >= 2:
                                    pe.wait_ge(max_rd, n * (H * T) + (v - 1))
                                mm(bank[tt % 2], qst[0:MROW, e, tt * P:(tt + 1) * P], kst[0:MROW, e, :],
                                   start=True, stop=True).then_inc(max_ps, 1)
                        if 0 <= s < H:
                            if s % 2 == 0:
                                p = s // 2
                                pe.wait_ge(mstack[p % 2], n * (4 * 16) + 16 * (p // 2 + 1))
                            for hf in range(2):
                                v = 2 * s + hf
                                if v >= 2:
                                    pe.wait_ge(exp_rd, n * (2 * H) + (v - 1))
                                for j in range(2):
                                    kt = 2 * hf + j
                                    i = mm(bank[2 + kt], kst[:, s, kt * P:(kt + 1) * P], qst[:, s, :], start=True, stop=True)
                                i.then_inc(exp_ps, 1)
                        if s >= G:
                            g, kt = s // G - 1, s % G
                            if kt == 0:
                                if g == 0:
                                    pe.wait_ge(v_sb, n * 2 + 2)
                                else:
                                    pe.wait_ge(oT_sb, n * NG + g)
                                pe.wait_ge(exp_rd, n * (2 * H) + 2 * G * (g + 1))
                            for j in range(G):
                                i = mm(bank[6][32 * j:32 * j + 32], vn[:, kt, G * g + j, :], probs[:, g % 2, kt, j, :],
                                       start=kt == 0, stop=kt == T - 1)
                            i.then_inc(pv_step, 1)
                        if (s + 3) % 2 == 0 and 0 <= (s + 3) // 2 < H // 2:
                            p = (s + 3) // 2
                            pe.wait_ge(msplit, n * (4 * (H // 2)) + 4 * (p + 1))
                            if p == 0:
                                pe.wait_ge(v_sb, n * 2 + 2)
                            else:
                                pe.wait_ge(mrow_sb, n * (H // 2) + p)
                            for tt in range(T):
                                i = nc.tensor.transpose(mrow_bank[0:2 * NMR, tt * P:(tt + 1) * P],
                                                        npart[:, p % 2, tt].rearrange("p a b c -> p (a b c)"), idb[:])
                            i.then_inc(mrow_ps, 1)
                    pe.wait_ge(oT_sb, n * NG + NG)
                    for tt in range(T):
                        for g in range(NG):
                            i = nc.tensor.transpose(bank[2 + tt][:, g * P:(g + 1) * P], oT[:, g, tt * P:(tt + 1) * P], idf[:])
                        i.then_inc(nat_ps, 1)
                    for k in range(KD):
                        for tt in range(T):
                            if k == 0:
                                pe.wait_ge(attn_sb, n * T + (tt + 1))
                            i = nc.tensor.transpose(bank[k][:, tt * P:(tt + 1) * P], h[:, tt, k * P:(k + 1) * P], idf[:])
                        i.then_inc(aT_ps, 1)
                    pe.wait_ge(aT_act, n + 1)
                    pe.wait_ge(aT_dve, n + 1)
                    for tt in range(T):
                        for k in range(KD):
                            i = mm(bank[2 + tt][:, 0:D], hT[:, k, tt * P:(tt + 1) * P], wo[l][:, k, :], start=k == 0, stop=k == KD - 1)
                        i.then_inc(res_ps, 1)
                    transposed(b, 2 * l + 1)
                    if l == 0:
                        for m in range(M0 + 3):
                            if m < M0:
                                if m >= 4:
                                    pe.wait_ge(relu_rd, b * M0 + (m - 3))
                                for k in range(KD):
                                    i = mm(bank[[2, 3, 0, 1][m % 4]], wfc[:, k, m * P:(m + 1) * P], hT[:, k, :], start=k == 0, stop=k == KD - 1)
                                i.then_inc(fc_ps, 1)
                            if m >= 3:
                                c = m - 3
                                pe.wait_ge(sq, b * M0 + (c + 1))
                                for tt in range(T):
                                    i = mm(bank[4 + tt][:, 0:D], r2[:, c, tt * P:(tt + 1) * P], wpr[:, c, :], start=c == 0, stop=c == M0 - 1)
                                    if c == M0 - 1:
                                        i.then_inc(res_ps, 1)
                    else:
                        for a in range(-1, PAR + 1):
                            if 0 <= a < PAR:
                                pe.wait_ge(dec_sb, b * PAR + (a + 1))
                                for leaf, rows in ((0, INNER), (1, LEAVES)):
                                    if a >= 1:
                                        pe.wait_ge(masked_sb, b * (2 * PAR) + (2 * (a - 1) + leaf + 1))
                                    mm(bank[2 + leaf][0:rows], anc[:, leaf * INNER:leaf * INNER + rows], dec[0:INNER, a % 2, :],
                                       start=True, stop=True).then_inc(sel_ps, 1)
                            if a >= 1:
                                c = a - 1
                                for leaf, rows in ((0, INNER), (1, LEAVES)):
                                    pe.wait_ge(masked_sb, b * (2 * PAR) + (2 * c + leaf + 1))
                                    for tt in range(T):
                                        i = mm(bank[4 + tt][:, 0:D], masked[0:rows, c % 2, leaf, tt * P:(tt + 1) * P],
                                               wout[0:rows, c, leaf, :], start=c == 0 and leaf == 0, stop=c == PAR - 1 and leaf == 1)
                                        if c == PAR - 1 and leaf == 1:
                                            i.then_inc(res_ps, 1)
                                        elif tt == T - 1:
                                            i.then_inc(fc_used, 1)
                            if a + 1 < PAR:
                                c = a + 1
                                for leaf, rows in ((0, INNER), (1, LEAVES)):
                                    if c >= 1:
                                        pe.wait_ge(lg_act, b * (2 * PAR) + 2 * c)
                                    for k in range(KD):
                                        i = mm(bank[leaf][0:rows], win[:, k, c, leaf * INNER:leaf * INNER + rows], hT[:, k, :],
                                               start=k == 0, stop=k == KD - 1)
                                    i.then_inc(lg_ps, 1)


def bits(c):
    return (c.view(np.uint32) >> 16).astype(np.uint16)


def constants():
    anc = np.zeros((INNER, NODES), np.float32)
    right = np.zeros(NODES, np.float32)
    for node in range(NODES):
        c = node
        while c:
            parent = (c - 1) // 2
            turn = c - 2 * parent - 1
            anc[parent, node] = 1.0 if turn else -1.0
            right[node] += turn
            c = parent
    thr = np.zeros((P, 2), np.float32)
    thr[:INNER, 0] = right[:INNER]
    thr[:LEAVES, 1] = right[INNER:]
    krows = np.zeros((NMR, H, S), np.float32)
    for r in range(NMR):
        blk = r % (S // BLK)
        krows[r, :, blk * BLK:(blk + 1) * BLK] = 1.0
    return {"anc": bits(anc), "thr": thr, "krows": bits(krows.reshape(NMR, H * S)),
            "idf": np.eye(P, dtype=np.float32), "idb": bits(np.eye(P, dtype=np.float32))}


def by_feature(w):
    return w.reshape(-1, H // HH, HH, HD).transpose(0, 1, 3, 2).reshape(-1, D)


def kernel(**inp):
    import concourse.bacc as _bacc
    from concourse.bass_utils import run_bass_kernel_spmd as _run

    a = {k: np.asarray(v) for k, v in inp.items()}
    qkv_b = a["L1_attn_qkv_b"]
    qkv_w = a["L1_attn_qkv_w"]
    b_in = a["L1_ffn_b_in"].reshape(PAR, NODES)
    bias_in = np.zeros((P, PAR, 2), b_in.dtype)
    bias_in[:INNER, :, 0] = b_in[:, :INNER].T
    bias_in[:LEAVES, :, 1] = b_in[:, INNER:].T
    data = {
        "x": a["L0_attn_hidden_states"],
        "wq0": by_feature(a["L0_attn_w_q"]), "wk0": by_feature(a["L0_attn_w_k"]), "wv0": a["L0_attn_w_v"], "wo0": a["L0_attn_w_o"],
        "wfcT": a["L0_ffn_w_fc"].T, "wprT": a["L0_ffn_w_proj"].T,
        "fast_b": a["L0_ffn_fast_b"], "uT": a["L0_ffn_u"].T, "v": a["L0_ffn_v"],
        "gate": np.broadcast_to(a["L0_ffn_gate"].reshape(1, 1), (P, 1)),
        "wqkvT": np.concatenate([by_feature(qkv_w[:D].T), by_feature(qkv_w[D:2 * D].T), qkv_w[2 * D:].T], 1), "wo1T": a["L1_attn_out_w"].T,
        "bqk": by_feature(qkv_b[:2 * D].reshape(2, D)).reshape(2, 2, P).transpose(2, 1, 0).reshape(P, 4),
        "bv": np.broadcast_to(np.tile(qkv_b[2 * D:], 2), (P, 2 * D)),
        "bo": np.broadcast_to(a["L1_attn_out_b"], (P, D)),
        "winT": a["L1_ffn_W_in"].T, "woutT": a["L1_ffn_W_out"].T,
        "bin": bias_in.reshape(P, PAR * 2),
    }
    data.update(constants())
    nc = _bacc.Bacc("TRN2", target_bir_lowering=False, num_devices=1, dynamic_dma_scratch_size=2048)
    arrays, t = {}, {}
    for name, v in data.items():
        arrays[f"in_{name}"] = np.ascontiguousarray(v)
        t[name] = nc.dram_tensor(f"in_{name}", v.shape, mybir.dt.from_np(v.dtype), kind="ExternalInput").ap()
    out = nc.dram_tensor("out_0", (B, S, D), F32, kind="ExternalOutput").ap()
    build(nc, t, out)
    r = _run(nc, [arrays], core_ids=[0])
    return r.results[0]["out_0"]
```

```python
import concourse.bass as bass
from concourse import mybir
from contextlib import ExitStack
import numpy as np

F32 = mybir.dt.float32
F16 = mybir.dt.float16
ACT = mybir.ActivationFunctionType
ALU = mybir.AluOpType
AX = mybir.AxisListType

P = 128
B, S, D = 16, 512, 256
T = S // P
KD = D // P
H = 16
HD = D // H
HH = P // HD
G = 4
NG = H // G
QSCALE = HD ** -0.5
BLK = 256
F0 = 1024
M0 = F0 // P
PAR, DEPTH = 8, 7
NODES = 2 ** (DEPTH + 1) - 1
INNER = 2 ** DEPTH - 1
LEAVES = NODES - INNER
EPS = 1e-5
RANK = 16

HI, LO = 0, 1
QPART = [HI, HI, LO]
KPART = [HI, LO, HI]
SLOTS = len(QPART)
WS = 64.0
MROW = 96
NMR = 3 * (S // BLK)
KROWS = MROW + NMR
LEAD = 5


def build(nc, t, out):
    ctx = ExitStack()
    with ctx:
        def sb(name, shape, dt=F32):
            return ctx.enter_context(nc.sbuf_tensor(name, shape, dt))

        def sem(name):
            return ctx.enter_context(nc.semaphore(name))

        xin = sb("xin", [P, T, D])
        x = sb("x", [P, T, D])
        h = sb("h", [P, T, D])
        hT = sb("hT", [P, 2, KD, S], F16)
        wq = [sb(f"wq{l}", [P, 2, KD, D], F16) for l in range(2)]
        wk = [sb(f"wk{l}", [P, 2, KD, D], F16) for l in range(2)]
        wv = [sb(f"wv{l}", [P, 2, KD, D], F16) for l in range(2)]
        wo = [sb(f"wo{l}", [P, 2, KD, D], F16) for l in range(2)]
        wfc = sb("wfc", [P, 2, KD, F0], F16)
        wpr = sb("wpr", [P, M0, D])
        win = sb("win", [P, 2, KD, PAR, NODES], F16)
        wout = sb("wout", [P, 2, PAR, 2, D], F16)
        bqk = sb("bqk", [P, 4])
        bv = sb("bv", [P, 1, D])
        bo = sb("bo", [P, D])
        bin_ = sb("bin_", [P, PAR, 2])
        binw = sb("binw", [P, PAR, 2])
        anc = sb("anc", [INNER, NODES], F16)
        thr = sb("thr", [P, 2])
        idf = sb("idf", [P, P])
        idb = sb("idb", [P, P], F16)
        gate = sb("gate", [P, 1])
        qst = sb("qst", [P, H, S], F16)
        kst = sb("kst", [P, H, S], F16)
        qk = sb("qk", [P, 4, S])
        parts = sb("parts", [P, 2, 4, S], F16)
        y = parts[:, 0, :, :].bitcast(F32)
        vn = sb("vn", [P, T, H, 2 * HD])
        probs = sb("probs", [P, 2, T, G, S])
        oT = qk
        nmax = sb("nmax", [P, 2, T, 2, 2])
        nres = sb("nres", [P, 2, T, 2, 2])
        npart = sb("npart", [P, 2, T, 3, 2, 2], F16)
        nrow = sb("nrow", [2 * NMR, 2, S], F16)
        rden = sb("rden", [P, T, H])
        stats = sb("stats", [P, T, 6])
        mean = sb("mean", [P, T])
        dif = sb("dif", [P, T])
        vpe = sb("vpe", [P, T])
        rstd = sb("rstd", [P, T])
        mhalf = sb("mhalf", [P, T])
        zero = sb("zero", [P, T, 2, 2])

        pr = probs[:].rearrange("p a b c s -> p (a b c) s")
        r2 = pr[:, 0:M0, :]
        rr = pr[:, M0:M0 + 4, :]
        actv = pr[:, 0:4, :].rearrange("p (a b) s -> p a b s", a=2)
        masked = pr[:, 4:8, :].rearrange("p (a b) s -> p a b s", a=2)
        mhi = pr[:, 8:10, :].bitcast(F16).rearrange("p a (b s) -> p a b s", b=2)
        mlo = pr[:, 10:12, :].bitcast(F16).rearrange("p a (b s) -> p a b s", b=2)
        dec = pr[:, 12:13, :].bitcast(F16).rearrange("p o (a s) -> p (o a) s", a=2)

        def flat(lo, hi):
            return pr[:, lo:hi, :].rearrange("p a s -> p (a s)")

        wabs, tgt, tlt, scl, hlf, nhl = flat(0, 4), flat(4, 8), flat(8, 12), flat(12, 14), flat(14, 16), flat(16, 18)
        fbs, uTs, vs, g1 = flat(18, 19)[0:RANK, 0:RANK], flat(19, 21)[0:RANK], flat(21, 22)[0:RANK, 0:D], flat(22, 24)[0:RANK]
        raw_attn = flat(24, 32).rearrange("p (w k n) -> p w k n", w=8, k=KD)
        raw_fc = qk[:].rearrange("p a s -> p (a s)").rearrange("p (k n) -> p k n", k=KD)
        raw_in = qst[:].rearrange("p a s -> p (a s)").bitcast(F32)[:, 0:KD * PAR * NODES].rearrange("p (k n) -> p k n", k=KD)
        raw_out = kst[:].rearrange("p a s -> p (a s)").bitcast(F32).rearrange("p (a l e) -> p a l e", a=PAR, l=2)
        onesf, onesp = h[:, 0, 0:P], h[:, 1, 0:P]

        ps = ctx.enter_context(nc.psum_tensor("ps", [P, 8, S], F32))
        bank = [ps[:, i, :] for i in range(8)]
        mrow_bank = bank[7].bitcast(F16)

        w_in = sem("w_in")
        abs_done = sem("abs_done")
        mean_ps = sem("mean_ps")
        tern = sem("tern")
        g1_ps = sem("g1_ps")
        g1_sb = sem("g1_sb")
        low_ps = sem("low_ps")
        ones_set = sem("ones_set")
        pool_set = sem("pool_set")
        w_hi = sem("w_hi")
        w_lo = sem("w_lo")
        stack_zero = sem("stack_zero")
        krows_in = sem("krows_in")
        x_in = sem("x_in")
        ln_stats = sem("ln_stats")
        ln_mv = sem("ln_mv")
        ln_rstd = sem("ln_rstd")
        ln_h = sem("ln_h")
        hT_ps = sem("hT_ps")
        hT_hi = sem("hT_hi")
        hT_lo = sem("hT_lo")
        xb_done = sem("xb_done")
        qk_ps = sem("qk_ps")
        v_ps = sem("v_ps")
        qk_sb = sem("qk_sb")
        qk_hi = sem("qk_hi")
        qk_lo = sem("qk_lo")
        v_sb = sem("v_sb")
        stack = [sem("stack0"), sem("stack1")]
        max_ps = sem("max_ps")
        max_rd = sem("max_rd")
        msplit = sem("msplit")
        mrow_ps = sem("mrow_ps")
        mrow_sb = sem("mrow_sb")
        mstack = [sem("mstack0"), sem("mstack1")]
        exp_ps = sem("exp_ps")
        exp_rd = sem("exp_rd")
        pv_step = sem("pv_step")
        oT_sb = sem("oT_sb")
        nat_ps = sem("nat_ps")
        rden_sb = sem("rden_sb")
        attn_sb = sem("attn_sb")
        aT_ps = sem("aT_ps")
        aT_hi = sem("aT_hi")
        aT_lo = sem("aT_lo")
        res_ps = sem("res_ps")
        x_upd = sem("x_upd")
        fc_ps = sem("fc_ps")
        relu_rd = sem("relu_rd")
        sq = sem("sq")
        lg_ps = sem("lg_ps")
        out_used = sem("out_used")
        lg_act = sem("lg_act")
        dec_sb = sem("dec_sb")
        sel_ps = sem("sel_ps")
        masked_sb = sem("masked_sb")
        mhi_sb = sem("mhi_sb")
        mlo_sb = sem("mlo_sb")
        y_sb = sem("y_sb")
        y_out = sem("y_out")

        block = ctx.enter_context(nc.Block())

        loads = [
            (raw_fc, t["wfcT"].rearrange("(k p) n -> p k n", p=P)),
            (wpr[:], t["wprT"].rearrange("(k p) n -> p k n", p=P)),
            (fbs, t["fast_b"]), (uTs, t["uT"]), (vs, t["v"]), (gate[:], t["gate"]),
            (idf[:], t["idf"]), (idb[:], t["idb"].bitcast(F16)),
            *((raw_attn[:, i], w.rearrange("(k p) n -> p k n", p=P)) for i, w in enumerate(
                (t["wq0"], t["wk0"], t["wv0"], t["wo0"], t["wqkvT"][:, 0:D], t["wqkvT"][:, D:2 * D], t["wqkvT"][:, 2 * D:3 * D], t["wo1T"]))),
            (raw_in, t["winT"].rearrange("(k p) n -> p k n", p=P)),
            (raw_out[0:INNER, :, 0, :], t["woutT"].rearrange("(a n) e -> n a e", n=NODES)[0:INNER]),
            (raw_out[0:LEAVES, :, 1, :], t["woutT"].rearrange("(a n) e -> n a e", n=NODES)[INNER:NODES]),
            (bqk[:], t["bqk"]), (bv[:], t["bv"].rearrange("p (a n) -> p a n", a=1)),
            (bo[:], t["bo"]),
            (bin_[:], t["bin"].rearrange("p (a n) -> p a n", n=2)),
            (anc[:], t["anc"].bitcast(F16)), (thr[:], t["thr"]),
        ]
        ALL_IN = 16 * (len(loads) - 1)

        w_parts = [(raw_attn[:, 4 * l + i], w[l][:, HI], w[l][:, LO]) for l in range(2) for i, w in enumerate((wq, wk, wv, wo))]
        w_parts += [
            (raw_in, *(win[:, p].rearrange("p k a n -> p k (a n)") for p in (HI, LO))),
            (raw_out[0:INNER, :, 0, :], wout[0:INNER, HI, :, 0, :], wout[0:INNER, LO, :, 0, :]),
            (raw_out[0:LEAVES, :, 1, :], wout[0:LEAVES, HI, :, 1, :], wout[0:LEAVES, LO, :, 1, :]),
            (raw_fc, wfc[:, HI], wfc[:, LO]),
        ]
        TERN = 20

        @block.sync
        def _(sp):
            for dst, src in loads[:-1]:
                sp.dma_start(dst, src).then_inc(w_in, 16)
            sp.dma_start(*loads[-1]).then_inc(y_out, 16)
            sp.wait_ge(stack_zero, 4)
            sp.dma_start(kst[MROW:KROWS, :, :], t["krows"].bitcast(F16).rearrange("r (a s) -> r a s", a=H)).then_inc(krows_in, 16)
            with sp.Fori(0, B) as b:
                sp.wait_ge(x_upd, 12 * b + 1)
                sp.dma_start(xin[:], t["x"][bass.ds(b, 1)].rearrange("o (t p) d -> p (o t) d", p=P)).then_inc(x_in, 16)
                for l in range(2):
                    n = b * 2 + l
                    for hf in range(2):
                        for part in (HI, LO):
                            for c, (dst, slots) in enumerate(((qst, QPART), (kst, KPART))):
                                sp.wait_ge((qk_hi, qk_lo)[part], n * 4 + (2 * hf + c + 1))
                                for s in range(SLOTS):
                                    if slots[s] == part:
                                        sp.dma_start(dst[s * HD:(s + 1) * HD, hf * HH:(hf + 1) * HH, :],
                                                     parts[:, part, 2 * hf + c, :]).then_inc(stack[hf], 16)
                    for p in range(H // 2):
                        sp.wait_ge(mrow_sb, n * (H // 2) + (p + 1))
                        sp.dma_start(qst[MROW:KROWS, 2 * p:2 * p + 2, :],
                                     nrow[:, p % 2, :]).then_inc(mstack[p % 2], 16)

        @block.gpsimd
        def _(pool):
            nc.gpsimd.memset(mhalf[:], -0.5).then_inc(pool_set, 1)
            nc.gpsimd.memset(zero[:], 0.0).then_inc(pool_set, 1)
            pool.wait_ge(pool_set, 2)

            def rstd_of(m):
                pool.wait_ge(ln_mv, m * 7 + 7)
                nc.gpsimd.tensor_tensor(rstd[:], vpe[:], mhalf[:], ALU.pow).then_inc(ln_rstd, 1)

            with pool.Fori(0, B) as b:
                for l in range(2):
                    n = b * 2 + l
                    rstd_of(b * 4 + 2 * l)
                    if l == 1:
                        pool.wait_ge(w_in, ALL_IN)
                        pool.wait_ge(ln_h, b * 4 * T + 3 * T)
                        nc.gpsimd.tensor_tensor(x[:], x[:], bo[:].rearrange("p (o d) -> p o d", o=1).to_broadcast([P, T, D]), ALU.add).then_inc(xb_done, 1)
                    for p in range(H // 2):
                        u = p % 2
                        pool.wait_ge(max_rd, n * (H * T) + (p + 1) * 2 * T)
                        if p >= 2:
                            pool.wait_ge(mrow_ps, n * (H // 2) + (p - 1))
                        a = nmax[:, u, :, :, :] if l == 0 else nmax[:, u, :, 0:1, :].to_broadcast([P, T, 2, 2])
                        q = npart[:, u, :, :, :, :]
                        k = n * (4 * (H // 2)) + 4 * p
                        nc.gpsimd.tensor_tensor(q[:, :, 0, :, :], a, zero[:], ALU.add).then_inc(msplit, 1)
                        pool.wait_ge(msplit, k + 1)
                        nc.gpsimd.tensor_tensor(nres[:, u], a, q[:, :, 0, :, :], ALU.subtract).then_inc(msplit, 1)
                        pool.wait_ge(msplit, k + 2)
                        nc.gpsimd.tensor_tensor(q[:, :, 1, :, :], nres[:, u], zero[:], ALU.add).then_inc(msplit, 1)
                        pool.wait_ge(msplit, k + 3)
                        nc.gpsimd.tensor_tensor(q[:, :, 2, :, :], nres[:, u], q[:, :, 1, :, :], ALU.subtract).then_inc(msplit, 1)
                    rstd_of(b * 4 + 2 * l + 1)
                    if l == 0:
                        for m in range(M0):
                            pool.wait_ge(relu_rd, b * M0 + (m + 1))
                            nc.gpsimd.tensor_tensor(r2[:, m, :], rr[:, m % 4, :], rr[:, m % 4, :], ALU.mult).then_inc(sq, 1)
                    else:
                        for a in range(PAR):
                            for leaf, rows in ((0, INNER), (1, LEAVES)):
                                pool.wait_ge(mhi_sb, b * (2 * PAR) + (2 * a + leaf + 1))
                                if a >= 2:
                                    pool.wait_ge(out_used, b * (2 * PAR - 1) + (2 * (a - 2) + leaf + 1))
                                nc.gpsimd.tensor_tensor(mlo[0:rows, a % 2, leaf, :], masked[0:rows, a % 2, leaf, :],
                                                        mhi[0:rows, a % 2, leaf, :], ALU.subtract).then_inc(mlo_sb, 1)

        @block.scalar
        def _(act):
            act.wait_ge(w_in, ALL_IN)
            nc.scalar.activation(wabs, raw_fc.rearrange("p k n -> p (k n)"), ACT.Abs).then_inc(abs_done, 1)
            act.wait_ge(mean_ps, 2)
            nc.scalar.activation(wabs, wpr[:].rearrange("p k n -> p (k n)"), ACT.Abs).then_inc(abs_done, 1)
            act.wait_ge(g1_ps, 2)
            nc.scalar.activation(g1, ps[0:RANK, 4:6, :].rearrange("p a s -> p (a s)"), ACT.Copy).then_inc(g1_sb, 1)
            for i, (raw, hi, lo) in enumerate(w_parts):
                if i == len(w_parts) - 1:
                    act.wait_ge(tern, TERN)
                nc.scalar.activation(hi, raw, ACT.Copy, scale=WS).then_inc(w_hi, 1)

            def hT_high(m):
                for k in range(KD):
                    act.wait_ge(hT_ps, m * KD + (k + 1))
                    nc.scalar.activation(hT[:, HI, k, :], bank[k], ACT.Copy).then_inc(hT_hi, 1)

            with act.Fori(0, B) as b:
                for l in range(2):
                    n = b * 2 + l
                    hT_high(b * 4 + 2 * l)
                    act.wait_ge(y_out, b * 16 + 16)
                    for c in range(4):
                        act.wait_ge(qk_ps, n * 4 + (c + 1))
                        scale = (1.0 if c % 2 else QSCALE) / WS
                        bias = bqk[:, c:c + 1] if l else 0.0
                        nc.scalar.activation(parts[:, HI, c, :], bank[2 + c], ACT.Identity, scale=scale, bias=bias).then_inc(qk_hi, 1)
                        nc.scalar.activation(qk[:, c, :], bank[2 + c], ACT.Identity, scale=scale, bias=bias).then_inc(qk_sb, 1)
                    for s in range(-2, H + G + 1):
                        for hf in range(2):
                            if hf == 0 and s % G == 0 and s >= 2 * G:
                                g = s // G - 2
                                act.wait_ge(pv_step, n * (4 * NG) + 4 * (g + 1))
                                nc.scalar.activation(oT[:, g, :], bank[6], ACT.Copy).then_inc(oT_sb, 1)
                            if hf == 1:
                                if s % 2 == 0 and (s + 2) // 2 < H // 2:
                                    p = (s + 2) // 2
                                    act.wait_ge(mrow_ps, n * (H // 2) + (p + 1))
                                    if p >= 2:
                                        act.wait_ge(mstack[p % 2], n * (4 * 16) + 16 * (p // 2))
                                    nc.scalar.activation(nrow[:, p % 2, :], mrow_bank[0:2 * NMR, 0:S], ACT.Copy).then_inc(mrow_sb, 1)
                            if 0 <= s < H:
                                g = s // G
                                if s % G == 0 and hf == 0 and g >= 2:
                                    act.wait_ge(pv_step, n * (4 * NG) + 4 * (g - 1))
                                act.wait_ge(exp_ps, n * (2 * H) + (2 * s + hf + 1))
                                nc.scalar.activation(probs[:, g % 2, 2 * hf:2 * hf + 2, s % G, :],
                                                     ps[:, 2 + 2 * hf:4 + 2 * hf, :], ACT.Exp).then_inc(exp_rd, 1)
                    for k in range(KD):
                        act.wait_ge(aT_ps, n * KD + (k + 1))
                        nc.scalar.activation(hT[:, HI, k, :], bank[k], ACT.Copy).then_inc(aT_hi, 1)
                    hT_high(b * 4 + 2 * l + 1)
                    if l == 0:
                        for m in range(M0):
                            act.wait_ge(fc_ps, b * M0 + (m + 1))
                            if m >= 4:
                                act.wait_ge(sq, b * M0 + (m - 3))
                            nc.scalar.activation(rr[:, m % 4, :], bank[[2, 3, 0, 1][m % 4]], ACT.Relu, scale=1.0 / WS).then_inc(relu_rd, 1)
                    else:
                        for a in range(PAR):
                            for leaf, rows in ((1, LEAVES), (0, INNER)):
                                if leaf:
                                    act.wait_ge(lg_ps, b * (2 * PAR) + (2 * a + 2))
                                    if a >= 2:
                                        act.wait_ge(masked_sb, b * (2 * PAR) + 2 * (a - 1))
                                else:
                                    act.wait_ge(dec_sb, b * PAR + (a + 1))
                                nc.scalar.activation(actv[0:rows, a % 2, leaf, :], bank[2 + leaf][0:rows], ACT.Silu, scale=1.0 / WS,
                                                     bias=bin_[0:rows, a, leaf:leaf + 1]).then_inc(lg_act, 1)
                            for leaf, rows in ((0, INNER), (1, LEAVES)):
                                act.wait_ge(masked_sb, b * (2 * PAR) + (2 * a + leaf + 1))
                                if a >= 2:
                                    act.wait_ge(out_used, b * (2 * PAR - 1) + (2 * (a - 2) + leaf + 1))
                                nc.scalar.activation(mhi[0:rows, a % 2, leaf, :], masked[0:rows, a % 2, leaf, :], ACT.Copy).then_inc(mhi_sb, 1)
                act.wait_ge(y_sb, b * T + T)
                act.dma_start(out[bass.ds(b, 1)].rearrange("o (t p) d -> p (o t) d", p=P), y).then_inc(y_out, 16)
            act.wait_ge(y_out, 16 * B + 16)

        @block.vector
        def _(dve):
            dve.wait_ge(w_in, ALL_IN)
            nc.vector.memset(onesf, 1.0 / D).then_inc(ones_set, 1)
            nc.vector.memset(onesp, 1.0 / F0).then_inc(ones_set, 1)
            nc.vector.memset(vn[:], 1.0).then_inc(ones_set, 1)
            nc.vector.memset(xin[:, 0, 0:1], 0.0).then_inc(x_upd, 1)
            nc.vector.tensor_scalar_mul(bqk[:, 0:4:2], bqk[:, 0:4:2], QSCALE).then_inc(ones_set, 1)
            nc.vector.tensor_scalar_mul(binw[:], bin_[:], WS).then_inc(ones_set, 1)
            step = 0

            def bitlinear(w, K, N, src, seen):
                nonlocal step
                wf = w
                v3 = lambda a: a[:, 0:K * N].rearrange("p (k n) -> p k n", k=K)
                bc = lambda a: a[:, 0:N].rearrange("p (o n) -> p o n", o=1).to_broadcast([P, K, N])
                dve.wait_ge(mean_ps, seen)
                for ins in (
                    lambda: nc.vector.tensor_scalar_max(scl[:, 0:N], src, 1e-5),
                    lambda: nc.vector.tensor_scalar_mul(hlf[:, 0:N], scl[:, 0:N], 0.5),
                    lambda: nc.vector.tensor_scalar_mul(nhl[:, 0:N], scl[:, 0:N], -0.5),
                    lambda: nc.vector.tensor_tensor(v3(tgt), wf, bc(hlf), ALU.is_gt),
                    lambda: nc.vector.tensor_tensor(v3(tlt), wf, bc(nhl), ALU.is_lt),
                    lambda: nc.vector.tensor_tensor(v3(tgt), v3(tgt), v3(tlt), ALU.subtract),
                    lambda: nc.vector.tensor_tensor(v3(tgt), v3(tgt), wf, ALU.subtract),
                    lambda: nc.vector.tensor_tensor(wf, wf, v3(tgt), ALU.add),
                    lambda: nc.vector.tensor_tensor(wf, wf, bc(scl), ALU.mult),
                ):
                    ins().then_inc(tern, 1)
                    step += 1
                    dve.wait_ge(tern, step)

            bitlinear(raw_fc, KD, F0, ps[:, 0:2, :].rearrange("p a s -> p (a s)"), 2)
            bitlinear(wpr[:], M0, D, bank[2][:, 0:D], 3)
            for k in range(KD):
                dve.wait_ge(low_ps, 2 * (k + 1))
                nc.vector.scalar_tensor_tensor(
                    raw_fc[:, k, :], ps[:, [0, 6][k]:[0, 6][k] + 2, :].rearrange("p a s -> p (a s)"), gate[:, 0:1],
                    raw_fc[:, k, :], ALU.mult, ALU.add).then_inc(tern, 1)
                step += 1
            assert step == TERN
            dve.wait_ge(tern, step)
            for i, (raw, hi, lo) in enumerate(w_parts):
                dve.wait_ge(w_hi, i + 1)
                nc.vector.scalar_tensor_tensor(lo, raw, WS, hi, ALU.mult, ALU.subtract).then_inc(w_lo, 1)
            dve.wait_ge(w_lo, len(w_parts))
            for st in (qst, kst):
                nc.vector.memset(st[32:64, :, :], 0.0).then_inc(stack_zero, 1)
                nc.vector.memset(st[64:MROW, :, :], 0.0).then_inc(stack_zero, 1)

            def stats_of(src, tt):
                nc.vector.bn_stats(stats[:, tt, :], src[:, tt, :]).then_inc(ln_stats, 1)

            def normalise(b, i, src):
                m = b * 4 + i
                even, odd = stats[:, :, 0:3], stats[:, :, 3:6]
                dve.wait_ge(ln_stats, m * T + T)
                nc.vector.tensor_tensor(mean[:], even[:, :, 1], odd[:, :, 1], ALU.add).then_inc(ln_mv, 1)
                nc.vector.tensor_tensor(dif[:], even[:, :, 1], odd[:, :, 1], ALU.subtract).then_inc(ln_mv, 1)
                nc.vector.tensor_tensor(vpe[:], even[:, :, 2], odd[:, :, 2], ALU.add).then_inc(ln_mv, 1)
                dve.wait_ge(ln_mv, m * 7 + 3)
                nc.vector.tensor_scalar(mean[:], mean[:], 0.5, None, ALU.mult).then_inc(ln_mv, 1)
                nc.vector.tensor_tensor(dif[:], dif[:], dif[:], ALU.mult).then_inc(ln_mv, 1)
                nc.vector.tensor_scalar(vpe[:], vpe[:], 1.0 / D, EPS, ALU.mult, ALU.add).then_inc(ln_mv, 1)
                dve.wait_ge(ln_mv, m * 7 + 6)
                nc.vector.scalar_tensor_tensor(vpe[:], dif[:], 0.25, vpe[:], ALU.mult, ALU.add).then_inc(ln_mv, 1)
                dve.wait_ge(ln_rstd, m + 1)
                for tt in range(T):
                    nc.vector.tensor_scalar(h[:, tt, :], src[:, tt, :], mean[:, tt:tt + 1], rstd[:, tt:tt + 1],
                                            ALU.subtract, ALU.mult).then_inc(ln_h, 1)
                for k in range(KD):
                    dve.wait_ge(hT_hi, m * KD + (k + 1))
                    nc.vector.tensor_tensor(hT[:, LO, k, :], bank[k], hT[:, HI, k, :], ALU.subtract).then_inc(hT_lo, 1)

            def residual(b, l, ffn, src):
                for tt in range(T):
                    dve.wait_ge(res_ps, b * (4 * T) + ((2 * l + ffn) * T + tt + 1))
                    nc.vector.scalar_tensor_tensor(x[:, tt, :], bank[(4 if ffn else 2) + tt][:, 0:D], 1.0 if ffn else 1.0 / WS,
                                                   src[:, tt, :], ALU.mult, ALU.add).then_inc(x_upd, 1)
                    dve.wait_ge(x_upd, b * 12 + ((2 * l + ffn) * T + tt + 2))
                    stats_of(x, tt)

            with dve.Fori(0, B) as b:
                for l in range(2):
                    n = b * 2 + l
                    if l == 0:
                        dve.wait_ge(x_in, b * 16 + 16)
                        for tt in range(T):
                            stats_of(xin, tt)
                    src = xin if l == 0 else x
                    normalise(b, 2 * l, src)
                    for c in range(4):
                        dve.wait_ge(qk_sb, n * 4 + (c + 1))
                        nc.vector.tensor_tensor(parts[:, LO, c, :], qk[:, c, :], parts[:, HI, c, :], ALU.subtract).then_inc(qk_lo, 1)
                    for tt in range(T):
                        if tt % 2 == 0:
                            dve.wait_ge(v_ps, n * 2 + (tt // 2 + 1))
                        dst = vn[:, tt, :, 0:HD]
                        sv = bank[6 + tt // 2][:, tt % 2 * D:(tt % 2 + 1) * D].rearrange("p (a d) -> p a d", d=HD)
                        if l == 0:
                            nc.vector.tensor_scalar_mul(dst, sv, 1.0 / WS).then_inc(v_sb, 1)
                        else:
                            nc.vector.scalar_tensor_tensor(dst, sv, 1.0 / WS, bv[:, 0, :].rearrange("p (a d) -> p a d", d=HD),
                                                           ALU.mult, ALU.add).then_inc(v_sb, 1)
                    for e in range(H):
                        p = e // 2
                        if e % 2 == 0 and p >= 2:
                            dve.wait_ge(msplit, n * (4 * (H // 2)) + 4 * (p - 1))
                        for tt in range(T):
                            dve.wait_ge(max_ps, n * (H * T) + (T * e + tt + 1))
                            src_ps = bank[tt % 2]
                            if l == 0:
                                nc.vector.tensor_reduce(nmax[:, p % 2, tt, :, e % 2], src_ps.rearrange("p (a s) -> p a s", s=BLK),
                                                        AX.X, ALU.max, negate=True).then_inc(max_rd, 1)
                            else:
                                nc.vector.tensor_reduce(nmax[:, p % 2, tt, 0, e % 2:e % 2 + 1], src_ps,
                                                        AX.X, ALU.max, negate=True).then_inc(max_rd, 1)
                    for tt in range(T):
                        nat = bank[2 + tt].rearrange("p (a c) -> p a c", c=2 * HD)
                        dve.wait_ge(nat_ps, n * T + (tt + 1))
                        nc.vector.reciprocal(rden[:, tt, :], nat[:, :, HD]).then_inc(rden_sb, 1)
                        dve.wait_ge(rden_sb, n * T + (tt + 1))
                        nc.vector.tensor_tensor(h[:, tt, :].rearrange("p (a d) -> p a d", d=HD), nat[:, :, 0:HD],
                                                rden[:, tt, :].rearrange("p (a o) -> p a o", o=1).to_broadcast([P, H, HD]),
                                                ALU.mult).then_inc(attn_sb, 1)
                    for k in range(KD):
                        dve.wait_ge(aT_hi, n * KD + (k + 1))
                        nc.vector.tensor_tensor(hT[:, LO, k, :], bank[k], hT[:, HI, k, :], ALU.subtract).then_inc(aT_lo, 1)
                    if l == 1:
                        dve.wait_ge(xb_done, b + 1)
                    residual(b, l, 0, src)
                    normalise(b, 2 * l + 1, x)
                    if l == 0:
                        residual(b, l, 1, x)
                    else:
                        for a in range(PAR):
                            dve.wait_ge(lg_ps, b * (2 * PAR) + (2 * a + 1))
                            if a >= 2:
                                dve.wait_ge(sel_ps, b * (2 * PAR) + 2 * (a - 1))
                            nc.vector.tensor_scalar(dec[0:INNER, a % 2, :], bank[2][0:INNER], binw[0:INNER, a, 0:1], 0.0,
                                                    ALU.add, ALU.is_gt).then_inc(dec_sb, 1)
                            for leaf, rows in ((0, INNER), (1, LEAVES)):
                                dve.wait_ge(sel_ps, b * (2 * PAR) + (2 * a + leaf + 1))
                                dve.wait_ge(lg_act, b * (2 * PAR) + (2 * a + 2))
                                if a >= 2:
                                    dve.wait_ge(mlo_sb, b * (2 * PAR) + (2 * (a - 2) + leaf + 1))
                                nc.vector.scalar_tensor_tensor(
                                    masked[0:rows, a % 2, leaf, :], bank[leaf][0:rows], thr[0:rows, leaf:leaf + 1],
                                    actv[0:rows, a % 2, leaf, :], ALU.is_equal, ALU.mult).then_inc(masked_sb, 1)
                        dve.wait_ge(y_out, b * 16 + 16)
                        for tt in range(T):
                            dve.wait_ge(res_ps, b * (4 * T) + (3 * T + tt + 1))
                            nc.vector.scalar_tensor_tensor(y[:, tt, :], bank[4 + tt][:, 0:D], 1.0 / WS, x[:, tt, :], ALU.mult, ALU.add).then_inc(y_sb, 1)

        @block.tensor
        def _(pe):
            mm = nc.tensor.matmul
            pe.wait_ge(w_in, ALL_IN)
            pe.wait_ge(ones_set, 5)
            pe.wait_ge(abs_done, 1)
            for j in range(2):
                for k in range(KD):
                    i = mm(bank[j], onesf, wabs[:, k * F0 + j * S:k * F0 + (j + 1) * S], start=k == 0, stop=k == KD - 1)
                i.then_inc(mean_ps, 1)
            pe.wait_ge(abs_done, 2)
            for k in range(M0):
                i = mm(bank[2][:, 0:D], onesp, wabs[:, k * D:(k + 1) * D], start=k == 0, stop=k == M0 - 1)
            i.then_inc(mean_ps, 1)
            for j in range(2):
                mm(bank[4 + j][0:RANK], fbs, uTs[:, j * S:(j + 1) * S], start=True, stop=True).then_inc(g1_ps, 1)
            pe.wait_ge(g1_sb, 1)
            pe.wait_ge(tern, 1)
            for k in range(KD):
                for j in range(2):
                    mm(bank[[0, 6][k] + j], vs[:, k * P:(k + 1) * P], g1[:, j * S:(j + 1) * S],
                       start=True, stop=True).then_inc(low_ps, 1)
            pe.wait_ge(w_lo, len(w_parts))
            pe.wait_ge(krows_in, 16)

            def product(out_ps, w, hf, width, before=None, moving=None):
                for k in range(KD):
                    for i, (a, c) in enumerate(((HI, HI), (LO, HI), (HI, LO))):
                        if before:
                            before(k, i)
                        if moving is None:
                            ins = mm(out_ps, w[:, a, k, hf:hf + width], hT[:, c, k, :], start=k + i == 0, stop=k == KD - 1 and i == 2)
                        else:
                            ins = mm(out_ps, hT[:, c, k, hf:hf + P], w[:, a, k, :], start=k + i == 0, stop=k == KD - 1 and i == 2)
                return ins

            def arrives(high, low, n):
                def before(k, i):
                    if i == 0:
                        pe.wait_ge(high, n * KD + (k + 1))
                    if i == 2:
                        pe.wait_ge(low, n * KD + (k + 1))
                return before

            def transposed(b, i):
                m = b * 4 + i
                for tt in range(T):
                    pe.wait_ge(ln_h, m * T + (tt + 1))
                    for k in range(KD):
                        ins = nc.tensor.transpose(bank[k][:, tt * P:(tt + 1) * P], h[:, tt, k * P:(k + 1) * P], idf[:])
                        if tt == T - 1:
                            ins.then_inc(hT_ps, 1)
                return arrives(hT_hi, hT_lo, m)

            with pe.Fori(0, B) as b:
                for l in range(2):
                    n = b * 2 + l
                    first = transposed(b, 2 * l)
                    for hf in range(2):
                        for w in (wq[l], wk[l]):
                            product(bank[2 + 2 * hf + (w is wk[l])], w, hf * P, P, first).then_inc(qk_ps, 1)
                            first = None
                    for tt in range(T):
                        i = product(bank[6 + tt // 2][:, tt % 2 * D:(tt % 2 + 1) * D], wv[l], tt * P, P, None, "tokens")
                        if tt % 2:
                            i.then_inc(v_ps, 1)
                    pe.wait_ge(qk_sb, n * 4 + 4)

                    def maxima(e, tt):
                        v = T * e + tt
                        if v >= 2:
                            pe.wait_ge(max_rd, n * (H * T) + (v - 1))
                        mm(bank[tt % 2], qst[0:MROW, e, tt * P:(tt + 1) * P], kst[0:MROW, e, :],
                           start=True, stop=True).then_inc(max_ps, 1)

                    def scores(s, hf):
                        v = 2 * s + hf
                        if v >= 2:
                            pe.wait_ge(exp_rd, n * (2 * H) + (v - 1))
                        for kt in (2 * hf, 2 * hf + 1):
                            i = mm(bank[2 + kt], kst[0:KROWS, s, kt * P:(kt + 1) * P], qst[0:KROWS, s, :], start=True, stop=True)
                        i.then_inc(exp_ps, 1)

                    for s in range(-LEAD, H + G):
                        e = s + LEAD
                        if e < H:
                            if e % HH == 0:
                                pe.wait_ge(stack[e // HH], n * (16 * 2 * SLOTS) + 16 * 2 * SLOTS)
                            maxima(e, 0)
                        if 0 <= s < H:
                            if s % 2 == 0:
                                p = s // 2
                                pe.wait_ge(mstack[p % 2], n * (4 * 16) + 16 * (p // 2 + 1))
                            scores(s, 0)
                        if e < H:
                            maxima(e, 1)
                        if 0 <= s < H:
                            scores(s, 1)
                        if e < H:
                            maxima(e, 2)
                        if s >= G:
                            g, kt = s // G - 1, s % G
                            if kt == 0:
                                if g == 0:
                                    pe.wait_ge(v_sb, n * T + T)
                                else:
                                    pe.wait_ge(oT_sb, n * NG + g)
                                pe.wait_ge(exp_rd, n * (2 * H) + 2 * G * (g + 1))
                            for j in range(G):
                                i = mm(bank[6][32 * j:32 * j + 32], vn[:, kt, G * g + j, :], probs[:, g % 2, kt, j, :],
                                       start=kt == 0, stop=kt == T - 1)
                            i.then_inc(pv_step, 1)
                        if e < H:
                            maxima(e, 3)
                        if (s + 3) % 2 == 0 and 0 <= (s + 3) // 2 < H // 2:
                            p = (s + 3) // 2
                            pe.wait_ge(msplit, n * (4 * (H // 2)) + 4 * (p + 1))
                            if p == 0:
                                pe.wait_ge(v_sb, n * T + T)
                            else:
                                pe.wait_ge(mrow_sb, n * (H // 2) + p)
                            for tt in range(T):
                                i = nc.tensor.transpose(mrow_bank[0:2 * NMR, tt * P:(tt + 1) * P],
                                                        npart[:, p % 2, tt].rearrange("p a b c -> p (a b c)"), idb[:])
                            i.then_inc(mrow_ps, 1)
                    pe.wait_ge(oT_sb, n * NG + NG)
                    for tt in range(T):
                        for g in range(NG):
                            i = nc.tensor.transpose(bank[2 + tt][:, g * P:(g + 1) * P], oT[:, g, tt * P:(tt + 1) * P], idf[:])
                        i.then_inc(nat_ps, 1)
                    for tt in range(T):
                        pe.wait_ge(attn_sb, n * T + (tt + 1))
                        for k in range(KD):
                            i = nc.tensor.transpose(bank[k][:, tt * P:(tt + 1) * P], h[:, tt, k * P:(k + 1) * P], idf[:])
                            if tt == T - 1:
                                i.then_inc(aT_ps, 1)
                    first = arrives(aT_hi, aT_lo, n)
                    for tt in range(T):
                        product(bank[2 + tt][:, 0:D], wo[l], tt * P, P, first, "tokens").then_inc(res_ps, 1)
                        first = None
                    first = transposed(b, 2 * l + 1)
                    if l == 0:
                        def project(c, tt):
                            i = mm(bank[4 + tt][:, 0:D], r2[:, c, tt * P:(tt + 1) * P], wpr[:, c, :], start=c == 0, stop=c == M0 - 1)
                            if c == M0 - 1:
                                i.then_inc(res_ps, 1)

                        for m in range(M0):
                            if m >= 4:
                                pe.wait_ge(relu_rd, b * M0 + (m - 3))
                            product(bank[[2, 3, 0, 1][m % 4]], wfc, m * P, P, first).then_inc(fc_ps, 1)
                            first = None
                            if m >= 3:
                                c = m - 3
                                pe.wait_ge(sq, b * M0 + (c + 1))
                                for tt in range(T):
                                    project(c, tt)
                        pe.wait_ge(sq, b * M0 + M0)
                        for tt in range(T):
                            for c in range(M0 - 3, M0):
                                project(c, tt)
                    else:
                        def leave(c, leaf, tt):
                            rows = (INNER, LEAVES)[leaf]
                            for i, (a, w) in enumerate(((mhi, HI), (mhi, LO), (mlo, HI))):
                                ins = mm(bank[4 + tt][:, 0:D], a[0:rows, c % 2, leaf, tt * P:(tt + 1) * P], wout[0:rows, w, c, leaf, :],
                                         start=c == 0 and leaf == 0 and i == 0, stop=c == PAR - 1 and leaf == 1 and i == 2)
                            return ins

                        for a in range(PAR + 1):
                            if a < PAR:
                                for leaf, rows in ((0, INNER), (1, LEAVES)):
                                    if a >= 1:
                                        pe.wait_ge(lg_act, b * (2 * PAR) + 2 * a)
                                    product(bank[2 + leaf][0:rows], win[:, :, :, a, :], leaf * INNER, rows, first).then_inc(lg_ps, 1)
                                    first = None
                            if a >= 2:
                                for leaf in range(2):
                                    pe.wait_ge(mlo_sb, b * (2 * PAR) + (2 * (a - 2) + leaf + 1))
                                    for tt in range(T):
                                        i = leave(a - 2, leaf, tt)
                                    i.then_inc(out_used, 1)
                            if a < PAR:
                                pe.wait_ge(dec_sb, b * PAR + (a + 1))
                                for leaf, rows in ((0, INNER), (1, LEAVES)):
                                    if a >= 1:
                                        pe.wait_ge(masked_sb, b * (2 * PAR) + (2 * (a - 1) + leaf + 1))
                                    mm(bank[leaf][0:rows], anc[:, leaf * INNER:leaf * INNER + rows], dec[0:INNER, a % 2, :],
                                       start=True, stop=True).then_inc(sel_ps, 1)
                        pe.wait_ge(mlo_sb, b * (2 * PAR) + 2 * PAR)
                        for tt in range(T):
                            i = leave(PAR - 1, 0, tt)
                            if tt == T - 1:
                                i.then_inc(out_used, 1)
                            leave(PAR - 1, 1, tt).then_inc(res_ps, 1)


def bits(c):
    return c.astype(np.float16).view(np.uint16)


def constants():
    anc = np.zeros((INNER, NODES), np.float32)
    right = np.zeros(NODES, np.float32)
    for node in range(NODES):
        c = node
        while c:
            parent = (c - 1) // 2
            turn = c - 2 * parent - 1
            anc[parent, node] = 1.0 if turn else -1.0
            right[node] += turn
            c = parent
    thr = np.zeros((P, 2), np.float32)
    thr[:INNER, 0] = right[:INNER]
    thr[:LEAVES, 1] = right[INNER:]
    krows = np.zeros((NMR, H, S), np.float32)
    for r in range(NMR):
        blk = r % (S // BLK)
        krows[r, :, blk * BLK:(blk + 1) * BLK] = 1.0
    return {"anc": bits(anc), "thr": thr, "krows": bits(krows.reshape(NMR, H * S)),
            "idf": np.eye(P, dtype=np.float32), "idb": bits(np.eye(P, dtype=np.float32))}


def by_feature(w):
    return w.reshape(-1, H // HH, HH, HD).transpose(0, 1, 3, 2).reshape(-1, D)


def kernel(**inp):
    import concourse.bacc as _bacc
    from concourse.bass_utils import run_bass_kernel_spmd as _run

    a = {k: np.asarray(v) for k, v in inp.items()}
    qkv_b = a["L1_attn_qkv_b"]
    qkv_w = a["L1_attn_qkv_w"]
    b_in = a["L1_ffn_b_in"].reshape(PAR, NODES)
    bias_in = np.zeros((P, PAR, 2), b_in.dtype)
    bias_in[:INNER, :, 0] = b_in[:, :INNER].T
    bias_in[:LEAVES, :, 1] = b_in[:, INNER:].T
    data = {
        "x": a["L0_attn_hidden_states"],
        "wq0": by_feature(a["L0_attn_w_q"]), "wk0": by_feature(a["L0_attn_w_k"]), "wv0": a["L0_attn_w_v"], "wo0": a["L0_attn_w_o"],
        "wfcT": a["L0_ffn_w_fc"].T, "wprT": a["L0_ffn_w_proj"].T,
        "fast_b": a["L0_ffn_fast_b"], "uT": a["L0_ffn_u"].T, "v": a["L0_ffn_v"],
        "gate": np.broadcast_to(a["L0_ffn_gate"].reshape(1, 1), (P, 1)),
        "wqkvT": np.concatenate([by_feature(qkv_w[:D].T), by_feature(qkv_w[D:2 * D].T), qkv_w[2 * D:].T], 1), "wo1T": a["L1_attn_out_w"].T,
        "bqk": by_feature(qkv_b[:2 * D].reshape(2, D)).reshape(2, 2, P).transpose(2, 1, 0).reshape(P, 4),
        "bv": np.broadcast_to(qkv_b[2 * D:], (P, D)),
        "bo": np.broadcast_to(a["L1_attn_out_b"], (P, D)),
        "winT": a["L1_ffn_W_in"].T, "woutT": a["L1_ffn_W_out"].T,
        "bin": bias_in.reshape(P, PAR * 2),
    }
    data.update(constants())
    nc = _bacc.Bacc("TRN2", target_bir_lowering=False, num_devices=1, dynamic_dma_scratch_size=2048)
    arrays, t = {}, {}
    for name, v in data.items():
        arrays[f"in_{name}"] = np.ascontiguousarray(v)
        t[name] = nc.dram_tensor(f"in_{name}", v.shape, mybir.dt.from_np(v.dtype), kind="ExternalInput").ap()
    out = nc.dram_tensor("out_0", (B, S, D), F32, kind="ExternalOutput").ap()
    build(nc, t, out)
    r = _run(nc, [arrays], core_ids=[0])
    return r.results[0]["out_0"]
```

```python
import concourse.bass as bass
from concourse import mybir
from contextlib import ExitStack
import numpy as np

F32 = mybir.dt.float32
F16 = mybir.dt.float16
ACT = mybir.ActivationFunctionType
ALU = mybir.AluOpType
AX = mybir.AxisListType

P = 128
B, S, D = 16, 512, 256
T = S // P
KD = D // P
H = 16
HD = D // H
HH = P // HD
G = 4
NG = H // G
QSCALE = HD ** -0.5
BLK = 256
F0 = 1024
M0 = F0 // P
PAR, DEPTH = 8, 7
NODES = 2 ** (DEPTH + 1) - 1
INNER = 2 ** DEPTH - 1
LEAVES = NODES - INNER
EPS = 1e-5
RANK = 16

HI, LO = 0, 1
QPART = [HI, HI, LO]
KPART = [HI, LO, HI]
SLOTS = len(QPART)
WS = 64.0
MROW = 96
NMR = 3 * (S // BLK)
KROWS = MROW + NMR


PAIR = 2
PAIRS = B // PAIR
PHASES = 8
ATT = {0: 0, 1: 1, 4: 2, 5: 3}
NATT = len(ATT)
UPD = 6
UNITS = PAIR * M0
TREES = PAIR * PAR
LEAD = {0: 5, 1: 6, 4: 5, 5: 6}
AHEAD = 15
NORM_AT = {11: 0, 12: 1, 13: 2, 15: 3}
LAST_MAX = H - 1 - LEAD[0]
T_AT, QK0_AT, V_AT, QK1_AT = LAST_MAX + 1, LAST_MAX + 2, LAST_MAX + 3, H - 1


def build(nc, t, out):
    ctx = ExitStack()
    with ctx:
        def sb(name, shape, dt=F32):
            return ctx.enter_context(nc.sbuf_tensor(name, shape, dt))

        def sem(name):
            return ctx.enter_context(nc.semaphore(name))

        x = [sb(f"x{q}", [P, T, D]) for q in range(PAIR)]
        h = sb("h", [P, T, D])
        hT = [sb(f"hT{i}", [P, 2, KD, S], F16) for i in range(PAIR)]
        wq = [sb(f"wq{l}", [P, 2, KD, D], F16) for l in range(2)]
        wk = [sb(f"wk{l}", [P, 2, KD, D], F16) for l in range(2)]
        wv = [sb(f"wv{l}", [P, 2, KD, D], F16) for l in range(2)]
        wo = [sb(f"wo{l}", [P, 2, KD, D], F16) for l in range(2)]
        wfc = sb("wfc", [P, 2, KD, F0], F16)
        wpr = sb("wpr", [P, M0, D])
        win = sb("win", [P, 2, KD, PAR, NODES], F16)
        wout = sb("wout", [P, 2, PAR, 2, D], F16)
        bqk = sb("bqk", [P, 4])
        bv = sb("bv", [P, 1, D])
        bo = sb("bo", [P, D])
        bin_ = sb("bin_", [P, PAR, 2])
        binw = sb("binw", [P, PAR, 2])
        anc = sb("anc", [INNER, NODES], F16)
        thr = sb("thr", [P, 2])
        idf = sb("idf", [P, P])
        idb = sb("idb", [P, P], F16)
        gate = sb("gate", [P, 1])
        qst = sb("qst", [P, H, S], F16)
        kst = sb("kst", [P, H, S], F16)
        qk = sb("qk", [P, 2, S])
        parts = sb("parts", [P, 2, 4, S], F16)
        vn = sb("vn", [P, 2, T, H, 2 * HD])
        probs = sb("probs", [P, 2, T, G, S])
        oT = sb("oT", [P, NG, S])
        nmax = sb("nmax", [P, 2, T, 2, 2])
        nres = sb("nres", [P, 2, T, 2, 2])
        npart = sb("npart", [P, 2, T, 3, 2, 2], F16)
        nrow = sb("nrow", [2 * NMR, 2, S], F16)
        rden = sb("rden", [P, T, H])
        stats = sb("stats", [P, T, 6])
        mean = sb("mean", [P, T])
        dif = sb("dif", [P, T])
        vpe = sb("vpe", [P, T])
        rstd = sb("rstd", [P, T])
        mhalf = sb("mhalf", [P, T])
        zero = sb("zero", [P, T, 2, 2])

        pr = probs[:].rearrange("p a b c s -> p (a b c) s")
        r2 = pr[:, 0:M0, :]
        rr = pr[:, M0:M0 + 4, :]
        actv = pr[:, 0:4, :].rearrange("p (a b) s -> p a b s", a=2)
        masked = pr[:, 4:8, :].rearrange("p (a b) s -> p a b s", a=2)
        mhi = pr[:, 8:10, :].bitcast(F16).rearrange("p a (b s) -> p a b s", b=2)
        mlo = pr[:, 10:12, :].bitcast(F16).rearrange("p a (b s) -> p a b s", b=2)
        dec = pr[:, 12:13, :].bitcast(F16).rearrange("p o (a s) -> p (o a) s", a=2)

        def flat(lo, hi):
            return pr[:, lo:hi, :].rearrange("p a s -> p (a s)")

        wabs, tgt, tlt, scl, hlf, nhl = flat(0, 4), flat(4, 8), flat(8, 12), flat(12, 14), flat(14, 16), flat(16, 18)
        fbs, uTs, vs, g1 = flat(18, 19)[0:RANK, 0:RANK], flat(19, 21)[0:RANK], flat(21, 22)[0:RANK, 0:D], flat(22, 24)[0:RANK]
        raw_attn = flat(24, 32).rearrange("p (w k n) -> p w k n", w=8, k=KD)
        raw_fc = oT[:].rearrange("p a s -> p (a s)").rearrange("p (k n) -> p k n", k=KD)
        raw_in = qst[:].rearrange("p a s -> p (a s)").bitcast(F32)[:, 0:KD * PAR * NODES].rearrange("p (k n) -> p k n", k=KD)
        raw_out = kst[:].rearrange("p a s -> p (a s)").bitcast(F32).rearrange("p (a l e) -> p a l e", a=PAR, l=2)
        onesf, onesp = h[:, 0, 0:P], h[:, 1, 0:P]

        ps = ctx.enter_context(nc.psum_tensor("ps", [P, 8, S], F32))
        bank = [ps[:, i, :] for i in range(8)]

        w_in = sem("w_in")
        abs_done = sem("abs_done")
        mean_ps = sem("mean_ps")
        tern = sem("tern")
        g1_ps = sem("g1_ps")
        g1_sb = sem("g1_sb")
        low_ps = sem("low_ps")
        ones_set = sem("ones_set")
        pool_set = sem("pool_set")
        w_hi = sem("w_hi")
        w_lo = sem("w_lo")
        stack_zero = sem("stack_zero")
        krows_in = sem("krows_in")
        x_in = [sem(f"x_in{q}") for q in range(PAIR)]
        ln_stats = sem("ln_stats")
        ln_mv = sem("ln_mv")
        ln_rstd = sem("ln_rstd")
        ln_h = sem("ln_h")
        hT_ps = sem("hT_ps")
        hT_hi = sem("hT_hi")
        hT_lo = sem("hT_lo")
        xb_done = sem("xb_done")
        qk_ps = sem("qk_ps")
        v_ps = sem("v_ps")
        qk_sb = sem("qk_sb")
        qk_hi = sem("qk_hi")
        qk_lo = sem("qk_lo")
        v_sb = sem("v_sb")
        stack = [sem("stack0"), sem("stack1")]
        max_ps = sem("max_ps")
        max_rd = sem("max_rd")
        msplit = sem("msplit")
        mrow_ps = sem("mrow_ps")
        mrow_sb = sem("mrow_sb")
        mstack = [sem("mstack0"), sem("mstack1")]
        exp_ps = sem("exp_ps")
        exp_rd = sem("exp_rd")
        pv_step = sem("pv_step")
        oT_sb = sem("oT_sb")
        nat_ps = sem("nat_ps")
        rden_sb = sem("rden_sb")
        attn_sb = sem("attn_sb")
        aT_ps = sem("aT_ps")
        aT_hi = sem("aT_hi")
        aT_lo = sem("aT_lo")
        proj_ps = sem("proj_ps")
        acc_ps = sem("acc_ps")
        x_upd = sem("x_upd")
        fc_ps = sem("fc_ps")
        relu_rd = sem("relu_rd")
        sq = sem("sq")
        lg_ps = sem("lg_ps")
        out_used = sem("out_used")
        lg_act = sem("lg_act")
        dec_sb = sem("dec_sb")
        sel_ps = sem("sel_ps")
        masked_sb = sem("masked_sb")
        mhi_sb = sem("mhi_sb")
        mlo_sb = sem("mlo_sb")
        y_sb = sem("y_sb")
        y_out = [sem(f"y_out{q}") for q in range(PAIR)]

        block = ctx.enter_context(nc.Block())

        loads = [
            (raw_fc, t["wfcT"].rearrange("(k p) n -> p k n", p=P)),
            (wpr[:], t["wprT"].rearrange("(k p) n -> p k n", p=P)),
            (fbs, t["fast_b"]), (uTs, t["uT"]), (vs, t["v"]), (gate[:], t["gate"]),
            (idf[:], t["idf"]), (idb[:], t["idb"].bitcast(F16)),
            *((raw_attn[:, i], w.rearrange("(k p) n -> p k n", p=P)) for i, w in enumerate(
                (t["wq0"], t["wk0"], t["wv0"], t["wo0"], t["wqkvT"][:, 0:D], t["wqkvT"][:, D:2 * D], t["wqkvT"][:, 2 * D:3 * D], t["wo1T"]))),
            (raw_in, t["winT"].rearrange("(k p) n -> p k n", p=P)),
            (raw_out[0:INNER, :, 0, :], t["woutT"].rearrange("(a n) e -> n a e", n=NODES)[0:INNER]),
            (raw_out[0:LEAVES, :, 1, :], t["woutT"].rearrange("(a n) e -> n a e", n=NODES)[INNER:NODES]),
            (bqk[:], t["bqk"]), (bv[:], t["bv"].rearrange("p (a n) -> p a n", a=1)),
            (bin_[:], t["bin"].rearrange("p (a n) -> p a n", n=2)),
            (anc[:], t["anc"].bitcast(F16)), (bo[:], t["bo"]), (thr[:], t["thr"]),
        ]
        ALL_IN = 16 * (len(loads) - PAIR)

        w_parts = [(raw_attn[:, 4 * l + i], w[l][:, HI], w[l][:, LO]) for l in range(2) for i, w in enumerate((wq, wk, wv, wo))]
        w_parts += [
            (raw_in, *(win[:, p].rearrange("p k a n -> p k (a n)") for p in (HI, LO))),
            (raw_out[0:INNER, :, 0, :], wout[0:INNER, HI, :, 0, :], wout[0:INNER, LO, :, 0, :]),
            (raw_out[0:LEAVES, :, 1, :], wout[0:LEAVES, HI, :, 1, :], wout[0:LEAVES, LO, :, 1, :]),
            (raw_fc, wfc[:, HI], wfc[:, LO]),
        ]
        TERN = 20

        def head_at(ph, i):
            return bank[(2 if ph in (0, PHASES - 1) else 0) + i]

        def max_at(ph, e, tt):
            if ph % 2 == 0 and e < LEAD[ph]:
                return bank[tt % 2]
            return bank[(0, 1, 7)[(e % 2 * (T + 1) + tt) % 3]]

        def mrow_at(ph, p):
            if p == H // 2 - 1:
                return bank[7].bitcast(F16)
            return bank[2 + p if ph % 2 == 0 and p < 2 else 1].bitcast(F16)

        HID = [m if m < 2 else 2 + m % 2 for m in range(UNITS)]

        def tree_summed(eng, b, a, leaf):
            if a % PAR == PAR - 1 and leaf == 1:
                eng.wait_ge(acc_ps, b * (4 * T) + (3 + a // PAR) * T)
            else:
                eng.wait_ge(out_used, b * (PAIR * (2 * PAR - 1)) + (2 * a + leaf + 1 - a // PAR))

        @block.sync
        def _(sp):
            for dst, src in loads[:-PAIR]:
                sp.dma_start(dst, src).then_inc(w_in, 16)
            for q in range(PAIR):
                sp.dma_start(*loads[len(loads) - PAIR + q]).then_inc(y_out[q], 16)
            sp.wait_ge(stack_zero, 4)
            sp.dma_start(kst[MROW:KROWS, :, :], t["krows"].bitcast(F16).rearrange("r (a s) -> r a s", a=H)).then_inc(krows_in, 16)

            def load(b, q, wrap):
                sp.wait_ge(y_out[q], b * 16 + 16)
                sp.dma_start(x[q][:], t["x"][bass.ds(wrap * PAIR + q, 1)].rearrange("o (t p) d -> p (o t) d", p=P)).then_inc(x_in[q], 16)

            def stack_up(m):
                for hf in range(2):
                    for part in (HI, LO):
                        for c, (dst, slots) in enumerate(((qst, QPART), (kst, KPART))):
                            sp.wait_ge((qk_hi, qk_lo)[part], m * 4 + (2 * hf + c + 1))
                            for s in range(SLOTS):
                                if slots[s] == part:
                                    sp.dma_start(dst[s * HD:(s + 1) * HD, hf * HH:(hf + 1) * HH, :],
                                                 parts[:, part, 2 * hf + c, :]).then_inc(stack[hf], 16)

            load(0, 0, 0)
            stack_up(0)
            load(0, 1, 0)
            with sp.Fori(0, PAIRS) as b:
                for n in range(NATT):
                    m = b * NATT + n
                    for p in range(H // 2):
                        sp.wait_ge(mrow_sb, m * (H // 2) + (p + 1))
                        sp.dma_start(qst[MROW:KROWS, 2 * p:2 * p + 2, :],
                                     nrow[:, p % 2, :]).then_inc(mstack[p % 2], 16)
                    if n == NATT - 1:
                        load(b + 1, 0, (b + 1) % PAIRS)
                    stack_up(m + 1)
                load(b + 1, 1, (b + 1) % PAIRS)
            for q in range(PAIR):
                sp.wait_ge(x_in[q], 16 * (PAIRS + 1))
                sp.wait_ge(stack[q], (16 * 2 * SLOTS) * (PAIRS * NATT + 1))

        @block.gpsimd
        def _(pool):
            nc.gpsimd.memset(mhalf[:], -0.5).then_inc(pool_set, 1)
            nc.gpsimd.memset(zero[:], 0.0).then_inc(pool_set, 1)
            pool.wait_ge(pool_set, 2)
            pool.wait_ge(w_in, ALL_IN)

            def rstd_of(b, ph):
                pool.wait_ge(ln_mv, (b * PHASES + ph) * 7 + 7)
                nc.gpsimd.tensor_tensor(rstd[:], vpe[:], mhalf[:], ALU.pow).then_inc(ln_rstd, 1)

            def qk_low(n, c):
                pool.wait_ge(qk_sb, n * 4 + (c + 1))
                nc.gpsimd.tensor_tensor(parts[:, LO, c, :], qk[:, c % 2, :], parts[:, HI, c, :], ALU.subtract).then_inc(qk_lo, 1)

            def split_maxima(b, ph, pairs=range(H // 2)):
                n, l = b * NATT + ATT[ph], ph // 4
                for p in pairs:
                    u = p % 2
                    pool.wait_ge(max_rd, n * (H * T) + (p + 1) * 2 * T)
                    if p >= 2:
                        pool.wait_ge(mrow_ps, n * (H // 2) + (p - 1))
                    a = nmax[:, u, :, :, :] if l == 0 else nmax[:, u, :, 0:1, :].to_broadcast([P, T, 2, 2])
                    q = npart[:, u, :, :, :, :]
                    k = n * (4 * (H // 2)) + 4 * p
                    nc.gpsimd.tensor_tensor(q[:, :, 0, :, :], a, zero[:], ALU.add).then_inc(msplit, 1)
                    pool.wait_ge(msplit, k + 1)
                    nc.gpsimd.tensor_tensor(nres[:, u], a, q[:, :, 0, :, :], ALU.subtract).then_inc(msplit, 1)
                    pool.wait_ge(msplit, k + 2)
                    nc.gpsimd.tensor_tensor(q[:, :, 1, :, :], nres[:, u], zero[:], ALU.add).then_inc(msplit, 1)
                    pool.wait_ge(msplit, k + 3)
                    nc.gpsimd.tensor_tensor(q[:, :, 2, :, :], nres[:, u], q[:, :, 1, :, :], ALU.subtract).then_inc(msplit, 1)
                    if p == 6:
                        rstd_of(b, ph + 1)
                    if l == 1 and p == 3:
                        pool.wait_ge(ln_h, b * (PHASES * T) + (ph + 1) * T)
                        nc.gpsimd.tensor_tensor(x[ph % 2][:], x[ph % 2][:], bo[:].rearrange("p (o d) -> p o d", o=1).to_broadcast([P, T, D]),
                                                ALU.add).then_inc(xb_done, 1)
                if ph + 1 in ATT and H // 2 - 1 in pairs:
                    for c in range(4):
                        qk_low(n + 1, c)

            rstd_of(0, 0)
            for c in range(4):
                qk_low(0, c)
            split_maxima(0, 0, (0,))
            with pool.Fori(0, PAIRS) as b:
                split_maxima(b, 0, range(1, H // 2))
                split_maxima(b, 1)
                rstd_of(b, 3)
                for m in range(UNITS):
                    pool.wait_ge(relu_rd, b * UNITS + (m + 1))
                    nc.gpsimd.tensor_tensor(r2[:, m % M0, :], rr[:, m % 4, :], rr[:, m % 4, :], ALU.mult).then_inc(sq, 1)
                    if m == M0 + 3:
                        rstd_of(b, 4)
                    if m == M0 + 5:
                        qk_low(b * NATT + 2, 0)
                        qk_low(b * NATT + 2, 1)
                qk_low(b * NATT + 2, 2)
                qk_low(b * NATT + 2, 3)
                split_maxima(b, 4)
                split_maxima(b, 5)
                for a in range(TREES):
                    for leaf, rows in ((0, INNER), (1, LEAVES)):
                        pool.wait_ge(mhi_sb, b * (2 * TREES) + (2 * a + leaf + 1))
                        if a >= 2:
                            tree_summed(pool, b, a - 2, leaf)
                        nc.gpsimd.tensor_tensor(mlo[0:rows, a % 2, leaf, :], masked[0:rows, a % 2, leaf, :],
                                                mhi[0:rows, a % 2, leaf, :], ALU.subtract).then_inc(mlo_sb, 1)
                    if a == 2:
                        rstd_of(b, 7)
                    if a == TREES - 6:
                        rstd_of(b + 1, 0)
                    if a == TREES - 3:
                        qk_low((b + 1) * NATT, 0)
                        qk_low((b + 1) * NATT, 1)
                    if a == TREES - 1:
                        qk_low((b + 1) * NATT, 2)
                        qk_low((b + 1) * NATT, 3)
                split_maxima(b + 1, 0, (0,))

        @block.scalar
        def _(act):
            act.wait_ge(w_in, ALL_IN)
            nc.scalar.activation(wabs, raw_fc.rearrange("p k n -> p (k n)"), ACT.Abs).then_inc(abs_done, 1)
            act.wait_ge(mean_ps, 2)
            nc.scalar.activation(wabs, wpr[:].rearrange("p k n -> p (k n)"), ACT.Abs).then_inc(abs_done, 1)
            act.wait_ge(g1_ps, 2)
            nc.scalar.activation(g1, ps[0:RANK, 4:6, :].rearrange("p a s -> p (a s)"), ACT.Copy).then_inc(g1_sb, 1)
            for i, (raw, hi, lo) in enumerate(w_parts):
                if i == len(w_parts) - 1:
                    act.wait_ge(tern, TERN)
                nc.scalar.activation(hi, raw, ACT.Copy, scale=WS).then_inc(w_hi, 1)

            def hT_high(b, ph):
                for k in range(KD):
                    act.wait_ge(hT_ps, (b * PHASES + ph) * KD + (k + 1))
                    nc.scalar.activation(hT[ph % 2][:, HI, k, :], head_at(ph, k), ACT.Copy).then_inc(hT_hi, 1)

            def qk_read(b, ph, c):
                n, l = b * NATT + ATT[ph], ph // 4
                act.wait_ge(qk_ps, n * 4 + (c + 1))
                scale = (1.0 if c % 2 else QSCALE) / WS
                bias = bqk[:, c:c + 1] if l else 0.0
                nc.scalar.activation(parts[:, HI, c, :], head_at(ph, c % 2), ACT.Identity, scale=scale, bias=bias).then_inc(qk_hi, 1)
                if c >= 2:
                    act.wait_ge(qk_lo, n * 4 + (c - 1))
                nc.scalar.activation(qk[:, c % 2, :], head_at(ph, c % 2), ACT.Identity, scale=scale, bias=bias).then_inc(qk_sb, 1)

            def values(b, ph):
                n = b * NATT + ATT[ph]
                for j in range(2):
                    act.wait_ge(v_ps, n * 2 + (j + 1))
                    nc.scalar.activation(vn[:, ph % 2, 2 * j:2 * j + 2, :, 0:HD].rearrange("p t a d -> p (t a) d"),
                                         head_at(ph, j).rearrange("p (a d) -> p a d", d=HD), ACT.Copy, scale=1.0 / WS).then_inc(v_sb, 2)

            def mrow_read(b, ph, p):
                n = b * NATT + ATT[ph]
                act.wait_ge(mrow_ps, n * (H // 2) + (p + 1))
                if p >= 2:
                    act.wait_ge(mstack[p % 2], n * (4 * 16) + 16 * (p // 2))
                nc.scalar.activation(nrow[:, p % 2, :], mrow_at(ph, p)[0:2 * NMR, 0:S], ACT.Copy).then_inc(mrow_sb, 1)

            def attention(b, ph):
                n = b * NATT + ATT[ph]
                for s in range(H + G + 1):
                    p = (s + LEAD[ph] - 1) // 2 - 1
                    if (s + LEAD[ph]) % 2 == 1 and p < H // 2:
                        mrow_read(b, ph, p)
                    if s == T_AT + 1:
                        hT_high(b, ph + 1)
                    if ph + 1 in ATT:
                        for c in {QK0_AT + 1: (0, 1), QK1_AT + 1: (2, 3)}.get(s, ()):
                            qk_read(b, ph + 1, c)
                        if s == V_AT + 1 and ph == 0:
                            values(b, ph + 1)
                        if s == AHEAD + 3:
                            mrow_read(b, ph + 1, 0)
                    if s % G == 0 and s >= 2 * G:
                        g = s // G - 2
                        act.wait_ge(pv_step, n * (4 * NG) + 4 * (g + 1))
                        nc.scalar.activation(oT[:, g, :], bank[6], ACT.Copy).then_inc(oT_sb, 1)
                    for hf in range(2):
                        if s < H:
                            g = s // G
                            if s % G == 0 and hf == 0 and g >= 2:
                                act.wait_ge(pv_step, n * (4 * NG) + 4 * (g - 1))
                            act.wait_ge(exp_ps, n * (2 * H) + (2 * s + hf + 1))
                            nc.scalar.activation(probs[:, g % 2, 2 * hf:2 * hf + 2, s % G, :],
                                                 ps[:, 2 + 2 * hf:4 + 2 * hf, :], ACT.Exp).then_inc(exp_rd, 1)
                if ph + 1 in ATT:
                    mrow_read(b, ph + 1, 1)
                for k in range(KD):
                    act.wait_ge(aT_ps, n * KD + (k + 1))
                    nc.scalar.activation(hT[ph % 2][:, HI, k, :], bank[2 + k], ACT.Copy).then_inc(aT_hi, 1)

            def send(b, q):
                act.wait_ge(y_sb, b * (PAIR * T) + (q + 1) * T)
                act.dma_start(out[bass.ds(b * PAIR + q, 1)].rearrange("o (t p) d -> p (o t) d", p=P), x[q][:]).then_inc(y_out[q], 16)

            hT_high(0, 0)
            qk_read(0, 0, 0)
            qk_read(0, 0, 1)
            values(0, 0)
            qk_read(0, 0, 2)
            qk_read(0, 0, 3)
            mrow_read(0, 0, 0)
            with act.Fori(0, PAIRS) as b:
                attention(b, 0)
                attention(b, 1)
                for m in range(UNITS):
                    act.wait_ge(fc_ps, b * UNITS + (m + 1))
                    if m >= 4:
                        act.wait_ge(sq, b * UNITS + (m - 3))
                    nc.scalar.activation(rr[:, m % 4, :], bank[HID[m]], ACT.Relu, scale=1.0 / WS).then_inc(relu_rd, 1)
                    if m == 3:
                        hT_high(b, 3)
                    if m == M0 + 4:
                        hT_high(b, 4)
                    if m == M0 + 5:
                        qk_read(b, 4, 0)
                        qk_read(b, 4, 1)
                qk_read(b, 4, 2)
                qk_read(b, 4, 3)
                mrow_read(b, 4, 0)
                attention(b, 4)
                attention(b, 5)
                for a in range(TREES):
                    for leaf, rows in ((1, LEAVES), (0, INNER)):
                        if leaf:
                            act.wait_ge(lg_ps, b * (2 * TREES) + (2 * a + 2))
                            if a >= 2:
                                act.wait_ge(masked_sb, b * (2 * TREES) + 2 * (a - 1))
                        else:
                            act.wait_ge(dec_sb, b * TREES + (a + 1))
                        nc.scalar.activation(actv[0:rows, a % 2, leaf, :], bank[leaf][0:rows], ACT.Silu, scale=1.0 / WS,
                                             bias=bin_[0:rows, a % PAR, leaf:leaf + 1]).then_inc(lg_act, 1)
                    if a == PAR - 1:
                        hT_high(b, 7)
                    if a == PAR + 2:
                        send(b, 0)
                    if a == TREES - 4:
                        hT_high(b + 1, 0)
                    if a == TREES - 3:
                        qk_read(b + 1, 0, 0)
                        qk_read(b + 1, 0, 1)
                    if a == TREES - 2:
                        values(b + 1, 0)
                    if a == TREES - 1:
                        qk_read(b + 1, 0, 2)
                        qk_read(b + 1, 0, 3)
                    for leaf, rows in ((0, INNER), (1, LEAVES)):
                        act.wait_ge(masked_sb, b * (2 * TREES) + (2 * a + leaf + 1))
                        if a >= 2:
                            tree_summed(act, b, a - 2, leaf)
                        nc.scalar.activation(mhi[0:rows, a % 2, leaf, :], masked[0:rows, a % 2, leaf, :], ACT.Copy).then_inc(mhi_sb, 1)
                send(b, 1)
                mrow_read(b + 1, 0, 0)
            for q in range(PAIR):
                act.wait_ge(y_out[q], 16 * PAIRS + 16)

        @block.vector
        def _(dve):
            dve.wait_ge(w_in, ALL_IN)
            nc.vector.memset(onesf, 1.0 / D).then_inc(ones_set, 1)
            nc.vector.memset(onesp, 1.0 / F0).then_inc(ones_set, 1)
            nc.vector.memset(vn[:], 1.0).then_inc(ones_set, 1)
            nc.vector.tensor_scalar_mul(bqk[:, 0:4:2], bqk[:, 0:4:2], QSCALE).then_inc(ones_set, 1)
            nc.vector.tensor_scalar_mul(binw[:], bin_[:], WS).then_inc(ones_set, 1)
            step = 0

            def bitlinear(w, K, N, src, seen):
                nonlocal step
                wf = w
                v3 = lambda a: a[:, 0:K * N].rearrange("p (k n) -> p k n", k=K)
                bc = lambda a: a[:, 0:N].rearrange("p (o n) -> p o n", o=1).to_broadcast([P, K, N])
                dve.wait_ge(mean_ps, seen)
                for ins in (
                    lambda: nc.vector.tensor_scalar_max(scl[:, 0:N], src, 1e-5),
                    lambda: nc.vector.tensor_scalar_mul(hlf[:, 0:N], scl[:, 0:N], 0.5),
                    lambda: nc.vector.tensor_scalar_mul(nhl[:, 0:N], scl[:, 0:N], -0.5),
                    lambda: nc.vector.tensor_tensor(v3(tgt), wf, bc(hlf), ALU.is_gt),
                    lambda: nc.vector.tensor_tensor(v3(tlt), wf, bc(nhl), ALU.is_lt),
                    lambda: nc.vector.tensor_tensor(v3(tgt), v3(tgt), v3(tlt), ALU.subtract),
                    lambda: nc.vector.tensor_tensor(v3(tgt), v3(tgt), wf, ALU.subtract),
                    lambda: nc.vector.tensor_tensor(wf, wf, v3(tgt), ALU.add),
                    lambda: nc.vector.tensor_tensor(wf, wf, bc(scl), ALU.mult),
                ):
                    ins().then_inc(tern, 1)
                    step += 1
                    dve.wait_ge(tern, step)

            bitlinear(raw_fc, KD, F0, ps[:, 0:2, :].rearrange("p a s -> p (a s)"), 2)
            bitlinear(wpr[:], M0, D, bank[2][:, 0:D], 3)
            for k in range(KD):
                dve.wait_ge(low_ps, 2 * (k + 1))
                nc.vector.scalar_tensor_tensor(
                    raw_fc[:, k, :], ps[:, [0, 6][k]:[0, 6][k] + 2, :].rearrange("p a s -> p (a s)"), gate[:, 0:1],
                    raw_fc[:, k, :], ALU.mult, ALU.add).then_inc(tern, 1)
                step += 1
            assert step == TERN
            dve.wait_ge(tern, step)
            for i, (raw, hi, lo) in enumerate(w_parts):
                dve.wait_ge(w_hi, i + 1)
                nc.vector.scalar_tensor_tensor(lo, raw, WS, hi, ALU.mult, ALU.subtract).then_inc(w_lo, 1)
            dve.wait_ge(w_lo, len(w_parts))
            for st in (qst, kst):
                nc.vector.memset(st[32:64, :, :], 0.0).then_inc(stack_zero, 1)
                nc.vector.memset(st[64:MROW, :, :], 0.0).then_inc(stack_zero, 1)

            def stats_of(q, tt):
                nc.vector.bn_stats(stats[:, tt, :], x[q][:, tt, :]).then_inc(ln_stats, 1)

            def arrived(b, q):
                dve.wait_ge(x_in[q], b * 16 + 16)
                for tt in range(T):
                    stats_of(q, tt)

            def norm_step(b, ph, step):
                m = b * PHASES + ph
                even, odd = stats[:, :, 0:3], stats[:, :, 3:6]
                if step == 0:
                    dve.wait_ge(ln_stats, m * T + T)
                    nc.vector.tensor_tensor(mean[:], even[:, :, 1], odd[:, :, 1], ALU.add).then_inc(ln_mv, 1)
                    nc.vector.tensor_tensor(dif[:], even[:, :, 1], odd[:, :, 1], ALU.subtract).then_inc(ln_mv, 1)
                    nc.vector.tensor_tensor(vpe[:], even[:, :, 2], odd[:, :, 2], ALU.add).then_inc(ln_mv, 1)
                if step == 1:
                    dve.wait_ge(ln_mv, m * 7 + 3)
                    nc.vector.tensor_scalar(mean[:], mean[:], 0.5, None, ALU.mult).then_inc(ln_mv, 1)
                    nc.vector.tensor_tensor(dif[:], dif[:], dif[:], ALU.mult).then_inc(ln_mv, 1)
                    nc.vector.tensor_scalar(vpe[:], vpe[:], 1.0 / D, EPS, ALU.mult, ALU.add).then_inc(ln_mv, 1)
                if step == 2:
                    dve.wait_ge(ln_mv, m * 7 + 6)
                    nc.vector.scalar_tensor_tensor(vpe[:], dif[:], 0.25, vpe[:], ALU.mult, ALU.add).then_inc(ln_mv, 1)
                if step == 3:
                    dve.wait_ge(ln_rstd, m + 1)
                    for tt in range(T):
                        nc.vector.tensor_scalar(h[:, tt, :], x[ph % 2][:, tt, :], mean[:, tt:tt + 1], rstd[:, tt:tt + 1],
                                                ALU.subtract, ALU.mult).then_inc(ln_h, 1)

            def normalise(b, ph):
                for step in range(4):
                    norm_step(b, ph, step)

            def hT_low(b, ph):
                for k in range(KD):
                    dve.wait_ge(hT_hi, (b * PHASES + ph) * KD + (k + 1))
                    nc.vector.tensor_tensor(hT[ph % 2][:, LO, k, :], head_at(ph, k), hT[ph % 2][:, HI, k, :], ALU.subtract).then_inc(hT_lo, 1)

            def residual(b, ph, tt, ffn):
                if ffn:
                    dve.wait_ge(acc_ps, b * (4 * T) + ((ph - 2) * T + tt + 1))
                    given, scale = bank[4 + tt][:, 0:D], 1.0
                else:
                    dve.wait_ge(proj_ps, (b * NATT + ATT[ph]) * 2 + (tt // 2 + 1))
                    given, scale = bank[4 + tt // 2][:, tt % 2 * D:(tt % 2 + 1) * D], 1.0 / WS
                nc.vector.scalar_tensor_tensor(x[ph % 2][:, tt, :], given, scale, x[ph % 2][:, tt, :], ALU.mult, ALU.add).then_inc(x_upd, 1)
                dve.wait_ge(x_upd, b * (UPD * T) + (ph * T + tt + 1))
                stats_of(ph % 2, tt)

            def values(b, ph):
                n = b * NATT + ATT[ph]
                for tt in range(T):
                    if tt % 2 == 0:
                        dve.wait_ge(v_ps, n * 2 + (tt // 2 + 1))
                    sv = head_at(ph, tt // 2)[:, tt % 2 * D:(tt % 2 + 1) * D].rearrange("p (a d) -> p a d", d=HD)
                    nc.vector.scalar_tensor_tensor(vn[:, ph % 2, tt, :, 0:HD], sv, 1.0 / WS, bv[:, 0, :].rearrange("p (a d) -> p a d", d=HD),
                                                   ALU.mult, ALU.add).then_inc(v_sb, 1)

            def maxima(b, ph, e):
                n, l, p = b * NATT + ATT[ph], ph // 4, e // 2
                if e % 2 == 0 and p >= 2:
                    dve.wait_ge(msplit, n * (4 * (H // 2)) + 4 * (p - 1))
                for tt in range(T):
                    dve.wait_ge(max_ps, n * (H * T) + (T * e + tt + 1))
                    if l == 0:
                        nc.vector.tensor_reduce(nmax[:, p % 2, tt, :, e % 2], max_at(ph, e, tt).rearrange("p (a s) -> p a s", s=BLK),
                                                AX.X, ALU.max, negate=True).then_inc(max_rd, 1)
                    else:
                        nc.vector.tensor_reduce(nmax[:, p % 2, tt, 0, e % 2:e % 2 + 1], max_at(ph, e, tt),
                                                AX.X, ALU.max, negate=True).then_inc(max_rd, 1)

            def attention(b, ph):
                n = b * NATT + ATT[ph]
                for e in range(LEAD[ph], H):
                    maxima(b, ph, e)
                    if e == min(NORM_AT) - 1 and ph == 0:
                        arrived(b, 1)
                    if e in NORM_AT:
                        norm_step(b, ph + 1, NORM_AT[e])
                hT_low(b, ph + 1)
                if ph + 1 in ATT:
                    if ph // 4 == 1:
                        values(b, ph + 1)
                    for e in range(LEAD[ph + 1] - 1):
                        maxima(b, ph + 1, e)
                for tt in range(T):
                    nat = bank[4 + tt % 2].rearrange("p (a c) -> p a c", c=2 * HD)
                    dve.wait_ge(nat_ps, n * T + (tt + 1))
                    nc.vector.reciprocal(rden[:, tt, :], nat[:, :, HD]).then_inc(rden_sb, 1)
                    dve.wait_ge(rden_sb, n * T + (tt + 1))
                    nc.vector.tensor_tensor(h[:, tt, :].rearrange("p (a d) -> p a d", d=HD), nat[:, :, 0:HD],
                                            rden[:, tt, :].rearrange("p (a o) -> p a o", o=1).to_broadcast([P, H, HD]),
                                            ALU.mult).then_inc(attn_sb, 1)
                for k in range(KD):
                    dve.wait_ge(aT_hi, n * KD + (k + 1))
                    nc.vector.tensor_tensor(hT[ph % 2][:, LO, k, :], bank[2 + k], hT[ph % 2][:, HI, k, :], ALU.subtract).then_inc(aT_lo, 1)
                if ph + 1 in ATT:
                    maxima(b, ph + 1, LEAD[ph + 1] - 1)
                if ph // 4 == 1:
                    dve.wait_ge(xb_done, b * PAIR + (ph % 2 + 1))
                for tt in range(T):
                    residual(b, ph, tt, False)

            def output(b, q):
                for tt in range(T):
                    dve.wait_ge(acc_ps, b * (4 * T) + ((2 + q) * T + tt + 1))
                    nc.vector.scalar_tensor_tensor(x[q][:, tt, :], bank[4 + tt][:, 0:D], 1.0 / WS, x[q][:, tt, :],
                                                   ALU.mult, ALU.add).then_inc(y_sb, 1)

            arrived(0, 0)
            normalise(0, 0)
            hT_low(0, 0)
            for e in range(LEAD[0]):
                maxima(0, 0, e)
            with dve.Fori(0, PAIRS) as b:
                attention(b, 0)
                attention(b, 1)
                normalise(b, 3)
                hT_low(b, 3)
                for tt in range(T):
                    residual(b, 2, tt, True)
                normalise(b, 4)
                hT_low(b, 4)
                values(b, 4)
                maxima(b, 4, 0)
                maxima(b, 4, 1)
                for tt in range(T):
                    residual(b, 3, tt, True)
                    if tt < 3:
                        maxima(b, 4, tt + 2)
                attention(b, 4)
                attention(b, 5)
                for a in range(TREES):
                    dve.wait_ge(lg_ps, b * (2 * TREES) + (2 * a + 1))
                    if a >= 2:
                        dve.wait_ge(sel_ps, b * (2 * TREES) + 2 * (a - 1))
                    nc.vector.tensor_scalar(dec[0:INNER, a % 2, :], bank[0][0:INNER], binw[0:INNER, a % PAR, 0:1], 0.0,
                                            ALU.add, ALU.is_gt).then_inc(dec_sb, 1)
                    if a == PAR - 1:
                        hT_low(b, 7)
                    if a == TREES - 4:
                        hT_low(b + 1, 0)
                    for leaf, rows in ((0, INNER), (1, LEAVES)):
                        dve.wait_ge(sel_ps, b * (2 * TREES) + (2 * a + leaf + 1))
                        dve.wait_ge(lg_act, b * (2 * TREES) + (2 * a + 2))
                        if a >= 2:
                            dve.wait_ge(mlo_sb, b * (2 * TREES) + (2 * (a - 2) + leaf + 1))
                        nc.vector.scalar_tensor_tensor(
                            masked[0:rows, a % 2, leaf, :], bank[2 + leaf][0:rows], thr[0:rows, leaf:leaf + 1],
                            actv[0:rows, a % 2, leaf, :], ALU.is_equal, ALU.mult).then_inc(masked_sb, 1)
                    if a == 3:
                        normalise(b, 7)
                    if a == PAR + 1:
                        output(b, 0)
                    if a == TREES - 5:
                        arrived(b + 1, 0)
                        normalise(b + 1, 0)
                for e in range(2):
                    maxima(b + 1, 0, e)
                output(b, 1)
                for e in range(2, LEAD[0]):
                    maxima(b + 1, 0, e)

        @block.tensor
        def _(pe):
            mm = nc.tensor.matmul
            pe.wait_ge(w_in, ALL_IN)
            pe.wait_ge(ones_set, 5)
            pe.wait_ge(abs_done, 1)
            for j in range(2):
                for k in range(KD):
                    i = mm(bank[j], onesf, wabs[:, k * F0 + j * S:k * F0 + (j + 1) * S], start=k == 0, stop=k == KD - 1)
                i.then_inc(mean_ps, 1)
            pe.wait_ge(abs_done, 2)
            for k in range(M0):
                i = mm(bank[2][:, 0:D], onesp, wabs[:, k * D:(k + 1) * D], start=k == 0, stop=k == M0 - 1)
            i.then_inc(mean_ps, 1)
            for j in range(2):
                mm(bank[4 + j][0:RANK], fbs, uTs[:, j * S:(j + 1) * S], start=True, stop=True).then_inc(g1_ps, 1)
            pe.wait_ge(g1_sb, 1)
            pe.wait_ge(tern, 1)
            for k in range(KD):
                for j in range(2):
                    mm(bank[[0, 6][k] + j], vs[:, k * P:(k + 1) * P], g1[:, j * S:(j + 1) * S],
                       start=True, stop=True).then_inc(low_ps, 1)
            pe.wait_ge(w_lo, len(w_parts))
            pe.wait_ge(krows_in, 16)

            def product(out_ps, w, hf, width, src, before=None, moving=None):
                for k in range(KD):
                    for i, (a, c) in enumerate(((HI, HI), (LO, HI), (HI, LO))):
                        if before:
                            before(k, i)
                        if moving is None:
                            ins = mm(out_ps, w[:, a, k, hf:hf + width], src[:, c, k, :], start=k + i == 0, stop=k == KD - 1 and i == 2)
                        else:
                            ins = mm(out_ps, src[:, c, k, hf:hf + P], w[:, a, k, :], start=k + i == 0, stop=k == KD - 1 and i == 2)
                return ins

            def transposed(b, ph):
                m = b * PHASES + ph
                for tt in range(T):
                    pe.wait_ge(ln_h, m * T + (tt + 1))
                    for k in range(KD):
                        ins = nc.tensor.transpose(head_at(ph, k)[:, tt * P:(tt + 1) * P], h[:, tt, k * P:(k + 1) * P], idf[:])
                        if tt == T - 1:
                            ins.then_inc(hT_ps, 1)

            def hT_ready(b, ph):
                pe.wait_ge(hT_hi, (b * PHASES + ph) * KD + KD)
                pe.wait_ge(hT_lo, (b * PHASES + ph) * KD + KD)

            def qk_unit(b, ph, c, before=0):
                n, l = b * NATT + ATT[ph], ph // 4
                if c == 0:
                    hT_ready(b, ph)
                if c >= 2:
                    pe.wait_ge(v_sb, n * T + 2 * (c - 1))
                    if before:
                        pe.wait_ge(max_rd, n * (H * T) + before * T)
                product(head_at(ph, c % 2), (wq, wk)[c % 2][l], c // 2 * P, P, hT[ph % 2]).then_inc(qk_ps, 1)

            def v_units(b, ph):
                n, l = b * NATT + ATT[ph], ph // 4
                for tt in range(T):
                    if tt % 2 == 0:
                        pe.wait_ge(qk_sb, n * 4 + (tt // 2 + 1))
                    i = product(head_at(ph, tt // 2)[:, tt % 2 * D:(tt % 2 + 1) * D], wv[l], tt * P, P, hT[ph % 2], None, "tokens")
                    if tt % 2:
                        i.then_inc(v_ps, 1)

            def maxima(b, ph, e, tt):
                n = b * NATT + ATT[ph]
                v = T * e + tt
                if v == 0 and ph % 2:
                    pe.wait_ge(v_sb, n * T + T)
                    pe.wait_ge(mrow_sb, n * (H // 2))
                if v == 0 and ph == 4:
                    pe.wait_ge(v_sb, n * T + T)
                if v == {0: 0, 4: T}.get(ph, T * (QK1_AT - AHEAD + 1)):
                    pe.wait_ge(qk_sb, n * 4 + 4)
                if e % HH == 0 and tt == 0:
                    pe.wait_ge(stack[e // HH], n * (16 * 2 * SLOTS) + 16 * 2 * SLOTS)
                if ph % 2 == 0 and e < LEAD[ph]:
                    last = v - 1
                elif e % 2 == 0:
                    last = v - 2
                else:
                    last = v - 1 if tt < 2 else v - 2
                    if tt == 2 and e >= 3 and (ph % 2 or e > LEAD[ph]):
                        pe.wait_ge(mrow_sb, n * (H // 2) + (e - 1) // 2)
                if last > 0:
                    pe.wait_ge(max_rd, n * (H * T) + last)
                mm(max_at(ph, e, tt), qst[0:MROW, e, tt * P:(tt + 1) * P], kst[0:MROW, e, :],
                   start=True, stop=True).then_inc(max_ps, 1)

            def maxima_row(b, ph, p):
                n = b * NATT + ATT[ph]
                pe.wait_ge(msplit, n * (4 * (H // 2)) + 4 * (p + 1))
                if ATT[ph] or p:
                    pe.wait_ge(mrow_sb, n * (H // 2) + p)
                if p == H // 2 - 1:
                    pe.wait_ge(max_rd, n * (H * T) + H * T)
                elif ph % 2 or p >= 2:
                    pe.wait_ge(max_rd, n * (H * T) + (2 * p + 2) * T + 2)
                for tt in range(T):
                    i = nc.tensor.transpose(mrow_at(ph, p)[0:2 * NMR, tt * P:(tt + 1) * P],
                                            npart[:, p % 2, tt].rearrange("p a b c -> p (a b c)"), idb[:])
                i.then_inc(mrow_ps, 1)

            def scores(b, ph, s, hf):
                n = b * NATT + ATT[ph]
                v = 2 * s + hf
                if v == 0 and ph % 2 == 0:
                    pe.wait_ge(mrow_sb, n * (H // 2) + 2)
                if v >= 2:
                    pe.wait_ge(exp_rd, n * (2 * H) + (v - 1))
                elif hf == 1 and ph > 0:
                    pe.wait_ge(x_upd, b * (UPD * T) + ph * T)
                for kt in (2 * hf, 2 * hf + 1):
                    i = mm(bank[2 + kt], kst[0:KROWS, s, kt * P:(kt + 1) * P], qst[0:KROWS, s, :], start=True, stop=True)
                i.then_inc(exp_ps, 1)

            def hidden(b, m):
                ph = 2 + m // M0
                if m % M0 == 0:
                    hT_ready(b, ph)
                if m >= 4:
                    pe.wait_ge(relu_rd, b * UNITS + (m - 1))
                product(bank[HID[m]], wfc, m % M0 * P, P, hT[ph % 2]).then_inc(fc_ps, 1)

            def logits(b, a, leaf):
                ph = 6 + a // PAR
                rows = (INNER, LEAVES)[leaf]
                if a % PAR == 0 and leaf == 0:
                    hT_ready(b, ph)
                if a >= 1:
                    pe.wait_ge(lg_act, b * (2 * TREES) + 2 * a)
                product(bank[leaf][0:rows], win[:, :, :, a % PAR, :], leaf * INNER, rows, hT[ph % 2]).then_inc(lg_ps, 1)

            def attention(b, ph):
                n, l, nxt = b * NATT + ATT[ph], ph // 4, ph + 1
                if ph == 4:
                    pe.wait_ge(x_upd, b * (UPD * T) + ph * T)
                if ph % 2 == 0:
                    maxima_row(b, ph, 1)
                for s in range(H + G):
                    e = s + LEAD[ph]
                    ahead = (ph, e) if e < H else (nxt, s - AHEAD) if s >= AHEAD and nxt in ATT else None
                    if ahead:
                        maxima(b, *ahead, 0)
                    if s < H:
                        if s % 2 == 0:
                            p = s // 2
                            pe.wait_ge(mstack[p % 2], n * (4 * 16) + 16 * (p // 2 + 1))
                        scores(b, ph, s, 0)
                    if ahead:
                        maxima(b, *ahead, 1)
                    if s < H:
                        scores(b, ph, s, 1)
                    if ahead:
                        maxima(b, *ahead, 2)
                    if s >= G:
                        g, kt = s // G - 1, s % G
                        if kt == 0:
                            if g == 0:
                                pe.wait_ge(v_sb, n * T + T)
                            else:
                                pe.wait_ge(oT_sb, n * NG + g)
                            pe.wait_ge(exp_rd, n * (2 * H) + 2 * G * (g + 1))
                        for j in range(G):
                            i = mm(bank[6][32 * j:32 * j + 32], vn[:, ph % 2, kt, G * g + j, :], probs[:, g % 2, kt, j, :],
                                   start=kt == 0, stop=kt == T - 1)
                        i.then_inc(pv_step, 1)
                    if ahead:
                        maxima(b, *ahead, 3)
                    if e % 2 == 0 and e // 2 - 1 < H // 2:
                        maxima_row(b, ph, e // 2 - 1)
                    if nxt in ATT and s in (AHEAD + 2, AHEAD + 4):
                        maxima_row(b, nxt, (s - AHEAD) // 2 - 1)
                    if s == T_AT:
                        pe.wait_ge(max_rd, n * (H * T) + H * T)
                        transposed(b, nxt)
                    if nxt in ATT:
                        for c in {QK0_AT: (0, 1), QK1_AT: (2, 3)}.get(s, ()):
                            qk_unit(b, nxt, c, QK1_AT - AHEAD + 1)
                        if s == V_AT:
                            v_units(b, nxt)

                def natural(tt):
                    if tt >= 2:
                        pe.wait_ge(attn_sb, n * T + (tt - 1))
                    for g in range(NG):
                        i = nc.tensor.transpose(bank[4 + tt % 2][:, g * P:(g + 1) * P], oT[:, g, tt * P:(tt + 1) * P], idf[:])
                    i.then_inc(nat_ps, 1)

                def aT_arrives(k, i):
                    if i == 0:
                        pe.wait_ge(aT_hi, n * KD + (k + 1))
                    if i == 2:
                        pe.wait_ge(aT_lo, n * KD + (k + 1))

                def projected(half):
                    for tt in (2 * half, 2 * half + 1):
                        i = product(bank[4 + half][:, tt % 2 * D:(tt % 2 + 1) * D], wo[l], tt * P, P, hT[ph % 2],
                                    None if tt else aT_arrives, "tokens")
                    i.then_inc(proj_ps, 1)

                pe.wait_ge(oT_sb, n * NG + NG)
                natural(0)
                natural(1)
                if nxt == 2:
                    hidden(b, 0)
                if nxt == 6:
                    logits(b, 0, 0)
                natural(2)
                natural(3)
                for tt in range(T):
                    pe.wait_ge(attn_sb, n * T + (tt + 1))
                    for k in range(KD):
                        i = nc.tensor.transpose(bank[2 + k][:, tt * P:(tt + 1) * P], h[:, tt, k * P:(k + 1) * P], idf[:])
                        if tt == T - 1:
                            i.then_inc(aT_ps, 1)
                if nxt == 2:
                    hidden(b, 1)
                if nxt == 6:
                    logits(b, 0, 1)
                if nxt in ATT:
                    maxima(b, nxt, LEAD[nxt] - 1, 0)
                    maxima(b, nxt, LEAD[nxt] - 1, 1)
                projected(0)
                if nxt in ATT:
                    maxima(b, nxt, LEAD[nxt] - 1, 2)
                    maxima(b, nxt, LEAD[nxt] - 1, 3)
                projected(1)

            def project(b, m, tt):
                c = m % M0
                i = mm(bank[4 + tt][:, 0:D], r2[:, c, tt * P:(tt + 1) * P], wpr[:, c, :], start=c == 0, stop=c == M0 - 1)
                if c == M0 - 1:
                    i.then_inc(acc_ps, 1)

            def leave(a, leaf, tt):
                c, rows = a % PAR, (INNER, LEAVES)[leaf]
                for i, (part, w) in enumerate(((mhi, HI), (mhi, LO), (mlo, HI))):
                    ins = mm(bank[4 + tt][:, 0:D], part[0:rows, a % 2, leaf, tt * P:(tt + 1) * P], wout[0:rows, w, c, leaf, :],
                             start=c == 0 and leaf == 0 and i == 0, stop=c == PAR - 1 and leaf == 1 and i == 2)
                return ins

            def tree_sum(b, a):
                if a == 0:
                    pe.wait_ge(x_upd, b * (UPD * T) + UPD * T)
                if a == PAR:
                    pe.wait_ge(y_sb, b * (PAIR * T) + T)
                for leaf in range(2):
                    pe.wait_ge(mlo_sb, b * (2 * TREES) + (2 * a + leaf + 1))
                    for tt in range(T):
                        i = leave(a, leaf, tt)
                        if a % PAR == PAR - 1 and leaf == 1:
                            i.then_inc(acc_ps, 1)
                    if not (a % PAR == PAR - 1 and leaf == 1):
                        i.then_inc(out_used, 1)

            transposed(0, 0)
            qk_unit(0, 0, 0)
            qk_unit(0, 0, 1)
            v_units(0, 0)
            qk_unit(0, 0, 2)
            qk_unit(0, 0, 3)
            for e in range(LEAD[0]):
                for tt in range(T):
                    maxima(0, 0, e, tt)
            maxima_row(0, 0, 0)
            with pe.Fori(0, PAIRS) as b:
                attention(b, 0)
                attention(b, 1)

                for m in range(2, UNITS + 1):
                    if m < UNITS:
                        hidden(b, m)
                    if m >= M0 + 7:
                        maxima(b, 4, m - M0 - 7, 0)
                        maxima(b, 4, m - M0 - 7, 1)
                    if m >= 3:
                        c = m - 3
                        pe.wait_ge(sq, b * UNITS + (c + 1))
                        if c % M0 == 0:
                            pe.wait_ge(x_upd, b * (UPD * T) + (2 + c // M0) * T)
                        for tt in range(T):
                            project(b, c, tt)
                        if m >= M0 + 7:
                            maxima(b, 4, m - M0 - 7, 2)
                            maxima(b, 4, m - M0 - 7, 3)
                    if m == 3:
                        pe.wait_ge(relu_rd, b * UNITS + 2)
                        transposed(b, 3)
                    if m == M0 + 4:
                        transposed(b, 4)
                    if m == M0 + 5:
                        qk_unit(b, 4, 0)
                        qk_unit(b, 4, 1)
                    if m == M0 + 6:
                        v_units(b, 4)
                    if m == M0 + 7:
                        qk_unit(b, 4, 2, 1)
                        qk_unit(b, 4, 3, 1)
                pe.wait_ge(sq, b * UNITS + UNITS)
                for tt in range(T):
                    for m in (UNITS - 2, UNITS - 1):
                        project(b, m, tt)
                    if tt < 3:
                        for j in range(T):
                            maxima(b, 4, tt + 2, j)
                    if tt == 0:
                        maxima_row(b, 4, 0)
                attention(b, 4)
                attention(b, 5)

                for a in range(TREES + 1):
                    if 0 < a < TREES:
                        logits(b, a, 0)
                        logits(b, a, 1)
                    if a == PAR - 1 or TREES - 4 <= a < TREES:
                        pe.wait_ge(masked_sb, b * (2 * TREES) + 2 * a)
                    if a == PAR - 1:
                        transposed(b, 7)
                    if a == TREES - 4:
                        transposed(b + 1, 0)
                    if a == TREES - 3:
                        qk_unit(b + 1, 0, 0)
                        qk_unit(b + 1, 0, 1)
                    if a == TREES - 2:
                        v_units(b + 1, 0)
                    if a == TREES - 1:
                        qk_unit(b + 1, 0, 2)
                        qk_unit(b + 1, 0, 3)
                    if a >= 2:
                        tree_sum(b, a - 2)
                    if a == PAR - 1:
                        hT_ready(b, 7)
                    if a == TREES - 4:
                        hT_ready(b + 1, 0)
                    if a == TREES - 3:
                        pe.wait_ge(qk_sb, (b + 1) * (NATT * 4) + 2)
                    if a == TREES - 2:
                        pe.wait_ge(v_sb, (b + 1) * (NATT * T) + T)
                    if a == TREES - 1:
                        pe.wait_ge(qk_sb, (b + 1) * (NATT * 4) + 4)
                    if a < TREES:
                        pe.wait_ge(dec_sb, b * TREES + (a + 1))
                        for leaf, rows in ((0, INNER), (1, LEAVES)):
                            if a >= 1:
                                pe.wait_ge(masked_sb, b * (2 * TREES) + (2 * (a - 1) + leaf + 1))
                            mm(bank[2 + leaf][0:rows], anc[:, leaf * INNER:leaf * INNER + rows], dec[0:INNER, a % 2, :],
                               start=True, stop=True).then_inc(sel_ps, 1)
                pe.wait_ge(lg_act, b * (2 * TREES) + 2 * TREES)
                for e in range(2):
                    for tt in range(T):
                        maxima(b + 1, 0, e, tt)
                tree_sum(b, TREES - 1)
                for e in range(2, LEAD[0]):
                    for tt in range(T):
                        maxima(b + 1, 0, e, tt)
                    if e == 2:
                        maxima_row(b + 1, 0, 0)
                pe.wait_ge(y_sb, b * (PAIR * T) + PAIR * T)


def bits(c):
    return c.astype(np.float16).view(np.uint16)


def constants():
    anc = np.zeros((INNER, NODES), np.float32)
    right = np.zeros(NODES, np.float32)
    for node in range(NODES):
        c = node
        while c:
            parent = (c - 1) // 2
            turn = c - 2 * parent - 1
            anc[parent, node] = 1.0 if turn else -1.0
            right[node] += turn
            c = parent
    thr = np.zeros((P, 2), np.float32)
    thr[:INNER, 0] = right[:INNER]
    thr[:LEAVES, 1] = right[INNER:]
    krows = np.zeros((NMR, H, S), np.float32)
    for r in range(NMR):
        blk = r % (S // BLK)
        krows[r, :, blk * BLK:(blk + 1) * BLK] = 1.0
    return {"anc": bits(anc), "thr": thr, "krows": bits(krows.reshape(NMR, H * S)),
            "idf": np.eye(P, dtype=np.float32), "idb": bits(np.eye(P, dtype=np.float32))}


def by_feature(w):
    return w.reshape(-1, H // HH, HH, HD).transpose(0, 1, 3, 2).reshape(-1, D)


def kernel(**inp):
    import concourse.bacc as _bacc
    from concourse.bass_utils import run_bass_kernel_spmd as _run

    a = {k: np.asarray(v) for k, v in inp.items()}
    qkv_b = a["L1_attn_qkv_b"]
    qkv_w = a["L1_attn_qkv_w"]
    b_in = a["L1_ffn_b_in"].reshape(PAR, NODES)
    bias_in = np.zeros((P, PAR, 2), b_in.dtype)
    bias_in[:INNER, :, 0] = b_in[:, :INNER].T
    bias_in[:LEAVES, :, 1] = b_in[:, INNER:].T
    data = {
        "x": a["L0_attn_hidden_states"],
        "wq0": by_feature(a["L0_attn_w_q"]), "wk0": by_feature(a["L0_attn_w_k"]), "wv0": a["L0_attn_w_v"], "wo0": a["L0_attn_w_o"],
        "wfcT": a["L0_ffn_w_fc"].T, "wprT": a["L0_ffn_w_proj"].T,
        "fast_b": a["L0_ffn_fast_b"], "uT": a["L0_ffn_u"].T, "v": a["L0_ffn_v"],
        "gate": np.broadcast_to(a["L0_ffn_gate"].reshape(1, 1), (P, 1)),
        "wqkvT": np.concatenate([by_feature(qkv_w[:D].T), by_feature(qkv_w[D:2 * D].T), qkv_w[2 * D:].T], 1), "wo1T": a["L1_attn_out_w"].T,
        "bqk": by_feature(qkv_b[:2 * D].reshape(2, D)).reshape(2, 2, P).transpose(2, 1, 0).reshape(P, 4),
        "bv": np.broadcast_to(qkv_b[2 * D:], (P, D)),
        "bo": np.broadcast_to(a["L1_attn_out_b"], (P, D)),
        "winT": a["L1_ffn_W_in"].T, "woutT": a["L1_ffn_W_out"].T,
        "bin": bias_in.reshape(P, PAR * 2),
    }
    data.update(constants())
    nc = _bacc.Bacc("TRN2", target_bir_lowering=False, num_devices=1, dynamic_dma_scratch_size=1024)
    arrays, t = {}, {}
    for name, v in data.items():
        arrays[f"in_{name}"] = np.ascontiguousarray(v)
        t[name] = nc.dram_tensor(f"in_{name}", v.shape, mybir.dt.from_np(v.dtype), kind="ExternalInput").ap()
    out = nc.dram_tensor("out_0", (B, S, D), F32, kind="ExternalOutput").ap()
    build(nc, t, out)
    r = _run(nc, [arrays], core_ids=[0])
    return r.results[0]["out_0"]
```
